# Optimizing a Trainium2 kernel written in Bass

```python
import numpy as np
import jax
import jax.numpy as jnp

def _softmax(x, axis=-1):
    return jax.nn.softmax(x, axis=axis)
def _gelu(x):
    return jax.nn.gelu(x, approximate=True)
def _silu(x):
    return jax.nn.silu(x)
def _sigmoid(x):
    return jax.nn.sigmoid(x)
def _layernorm(x, axis=-1, eps=1e-5):
    m = jnp.mean(x, axis=axis, keepdims=True)
    v = jnp.var(x, axis=axis, keepdims=True)
    return (x - m) / jnp.sqrt(v + eps)
def _scatter_add(tgt, idx, src, axis=0):
    return tgt.at[idx].add(src)
def _segment_sum(src, seg, n):
    return jax.ops.segment_sum(src, seg, n)

kernel_name = 'mk_conv_preact_d2_conv_nchw192_2dbabe'

def setup_inputs(seed: int = 0):
    np.random.seed(seed)
    _w = jnp.asarray
    def _rec_inputs():
        import jax
        import jax.numpy as jnp
        _gk = jax.random.key(seed)
        x = -0.0002221 + 1 * jax.random.normal(jax.random.fold_in(_gk, 1), (8, 192, 128, 128), jnp.float32)
        return x
    x = _rec_inputs()
    def _L0_conv_setup():
        import jax, jax.numpy as jnp
        import numpy as np
        B, C, H, W = (8, 192, 128, 128)
        NH, WS, PS = (6, 8, 8)
        HD = C // NH
        SCALE = HD ** (-0.5)

        def _rel_pos_log(ws):
            coords = np.stack(np.meshgrid(np.arange(ws), np.arange(ws), indexing='ij'))
            cf = coords.reshape(2, -1)
            rp = (cf[:, :, None] - cf[:, None, :]).transpose(1, 2, 0).astype(np.float32)
            return jnp.asarray(np.sign(rp) * np.log1p(np.abs(rp)))
        key = jax.random.key(seed)
        ks = jax.random.split(key, 8)
        s = 0.02
        return {'x': jax.random.normal(ks[0], (B, C, H, W), jnp.float32), 'V_w': jax.random.normal(ks[1], (C, C), jnp.float32) * s, 'V_b': jnp.zeros((C,), jnp.float32), 'QK_w': jax.random.normal(ks[2], (2 * C, C), jnp.float32) * s, 'QK_b': jnp.zeros((2 * C,), jnp.float32), 'proj_w': jax.random.normal(ks[3], (C, C), jnp.float32) * s, 'proj_b': jnp.zeros((C,), jnp.float32), 'meta_w1': jax.random.normal(ks[4], (2, 256), jnp.float32) * s, 'meta_b1': jnp.zeros((256,), jnp.float32), 'meta_w2': jax.random.normal(ks[5], (256, NH), jnp.float32) * s, 'meta_b2': jnp.zeros((NH,), jnp.float32)}
    _L0_conv_all = _L0_conv_setup()
    _L0_conv_in = {k: v for k, v in _L0_conv_all.items() if k in ('V_w', 'V_b', 'QK_w', 'QK_b', 'proj_w', 'proj_b', 'meta_w1', 'meta_b1', 'meta_w2', 'meta_b2', )}
    del _L0_conv_all

    def _L1_conv_setup():
        import jax, jax.numpy as jnp
        from jax import lax
        import numpy as np
        B, C, H, W = (16, 192, 128, 128)
        key = jax.random.key(seed)
        k1, k2, k3 = jax.random.split(key, 3)
        x = jax.random.normal(k1, (B, C, H, W), dtype=jnp.float32)
        fan_in = C
        bound = 1.0 / np.sqrt(fan_in)
        merge_w = jax.random.uniform(k2, (C, C, 1, 1), dtype=jnp.float32, minval=-bound, maxval=bound)
        merge_b = jax.random.uniform(k3, (C,), dtype=jnp.float32, minval=-bound, maxval=bound)
        return {'x': x, 'merge_w': merge_w, 'merge_b': merge_b}
    _L1_conv_all = _L1_conv_setup()
    _L1_conv_in = {k: v for k, v in _L1_conv_all.items() if k in ('merge_w', 'merge_b', )}
    del _L1_conv_all

    return {
        "x": x,
        "L0_conv_V_w": _L0_conv_in["V_w"],
        "L0_conv_V_b": _L0_conv_in["V_b"],
        "L0_conv_QK_w": _L0_conv_in["QK_w"],
        "L0_conv_QK_b": _L0_conv_in["QK_b"],
        "L0_conv_proj_w": _L0_conv_in["proj_w"],
        "L0_conv_proj_b": _L0_conv_in["proj_b"],
        "L0_conv_meta_w1": _L0_conv_in["meta_w1"],
        "L0_conv_meta_b1": _L0_conv_in["meta_b1"],
        "L0_conv_meta_w2": _L0_conv_in["meta_w2"],
        "L0_conv_meta_b2": _L0_conv_in["meta_b2"],
        "L1_conv_merge_w": _L1_conv_in["merge_w"],
        "L1_conv_merge_b": _L1_conv_in["merge_b"],
    }

def reference(x, L0_conv_V_w, L0_conv_V_b, L0_conv_QK_w, L0_conv_QK_b, L0_conv_proj_w, L0_conv_proj_b, L0_conv_meta_w1, L0_conv_meta_b1, L0_conv_meta_w2, L0_conv_meta_b2, L1_conv_merge_w, L1_conv_merge_b):
    import jax
    import jax.numpy as jnp
    def _L0_conv_ref(x, V_w, V_b, QK_w, QK_b, proj_w, proj_b, meta_w1, meta_b1, meta_w2, meta_b2):
        import jax, jax.numpy as jnp
        import numpy as np
        B, C, H, W = (8, 192, 128, 128)
        NH, WS, PS = (6, 8, 8)
        HD = C // NH
        SCALE = HD ** (-0.5)

        def _rel_pos_log(ws):
            coords = np.stack(np.meshgrid(np.arange(ws), np.arange(ws), indexing='ij'))
            cf = coords.reshape(2, -1)
            rp = (cf[:, :, None] - cf[:, None, :]).transpose(1, 2, 0).astype(np.float32)
            return jnp.asarray(np.sign(rp) * np.log1p(np.abs(rp)))
        N = WS * WS
        v = jnp.einsum('bchw,oc->bohw', x, V_w) + V_b[None, :, None, None]
        qk = jnp.einsum('bchw,oc->bohw', x, QK_w) + QK_b[None, :, None, None]
        qkv = jnp.concatenate([qk, v], axis=1)
        t = qkv.transpose(0, 2, 3, 1).reshape(B, H // WS, WS, W // WS, WS, 3 * C)
        wins = t.transpose(0, 1, 3, 2, 4, 5).reshape(-1, N, 3 * C)
        B_ = wins.shape[0]
        qkv3 = wins.reshape(B_, N, 3, NH, HD).transpose(2, 0, 3, 1, 4)
        q, k, vv = (qkv3[0] * SCALE, qkv3[1], qkv3[2])
        cg = N // (PS * PS)
        qp = q.reshape(B_, NH, cg, PS, PS, HD).transpose(0, 1, 2, 5, 3, 4)
        kp = k.reshape(B_, NH, cg, PS, PS, HD).transpose(0, 1, 2, 5, 3, 4)
        o = jnp.fft.irfft2(jnp.fft.rfft2(qp) * jnp.fft.rfft2(kp), s=(PS, PS))
        o = o.transpose(0, 1, 2, 4, 5, 3).reshape(B_, NH, N, HD)
        rp = _rel_pos_log(WS)
        bias = jax.nn.relu(rp @ meta_w1 + meta_b1) @ meta_w2 + meta_b2
        bias = bias.transpose(2, 0, 1)
        attn = jnp.einsum('bhnd,bhmd->bhnm', o, vv) + bias[None]
        attn = jax.nn.softmax(attn, axis=-1)
        y = jnp.einsum('bhnm,bhmd->bhnd', attn, vv).transpose(0, 2, 1, 3).reshape(B_, N, C)
        y = y.reshape(B, H // WS, W // WS, WS, WS, C).transpose(0, 1, 3, 2, 4, 5).reshape(B, H, W, C)
        y = y.transpose(0, 3, 1, 2)
        return jnp.einsum('bchw,oc->bohw', y, proj_w) + proj_b[None, :, None, None]

    def _L1_conv_ref(x, merge_w, merge_b):
        import jax, jax.numpy as jnp
        from jax import lax
        import numpy as np
        B, C, H, W = (16, 192, 128, 128)
        c = x.shape[1]
        dn = lax.conv_dimension_numbers(x.shape, (c, 1, 3, 3), ('NCHW', 'OIHW', 'NCHW'))
        lap = jnp.array([[0.0, -1.0, 0.0], [-1.0, 4.0, -1.0], [0.0, -1.0, 0.0]], dtype=x.dtype)
        lap_k = jnp.broadcast_to(lap.reshape(1, 1, 3, 3), (c, 1, 3, 3))
        edges = lax.conv_general_dilated(x, lap_k, window_strides=(1, 1), padding=((1, 1), (1, 1)), dimension_numbers=dn, feature_group_count=c)
        out = x + edges
        dn1 = lax.conv_dimension_numbers(out.shape, merge_w.shape, ('NCHW', 'OIHW', 'NCHW'))
        y = lax.conv_general_dilated(out, merge_w, window_strides=(1, 1), padding='VALID', dimension_numbers=dn1)
        return y + merge_b[None, :, None, None]

    def _gn(v, G=32, eps=1e-5):
        B_, C_, H_, W_ = v.shape
        g = v.reshape(B_, G, C_ // G, H_, W_)
        m = jnp.mean(g, axis=(2, 3, 4), keepdims=True)
        s = jnp.var(g, axis=(2, 3, 4), keepdims=True)
        return ((g - m) / jnp.sqrt(s + eps)).reshape(v.shape)

    def _ln_c(v, eps=1e-6):
        m = jnp.mean(v, axis=1, keepdims=True)
        s = jnp.var(v, axis=1, keepdims=True)
        return (v - m) / jnp.sqrt(s + eps)

    def _ln_t(v, eps=1e-5):
        m = jnp.mean(v, axis=-1, keepdims=True)
        s = jnp.var(v, axis=-1, keepdims=True)
        return (v - m) / jnp.sqrt(s + eps)

    def _to_tokens(v):
        B_, C_, H_, W_ = v.shape
        return v.reshape(B_, C_, H_ * W_).transpose(0, 2, 1)
    def _from_tokens(t, like):
        B_, C_, H_, W_ = like.shape
        return t.transpose(0, 2, 1).reshape(B_, C_, H_, W_)

    x = x + _L0_conv_ref(_gn(x), L0_conv_V_w, L0_conv_V_b, L0_conv_QK_w, L0_conv_QK_b, L0_conv_proj_w, L0_conv_proj_b, L0_conv_meta_w1, L0_conv_meta_b1, L0_conv_meta_w2, L0_conv_meta_b2)
    x = x + _L1_conv_ref(_gn(x), L1_conv_merge_w, L1_conv_merge_b)
    return x


_drawn_inputs = setup_inputs


def setup_inputs(seed=0):
    import zlib

    import numpy as np

    out = dict(_drawn_inputs(seed))
    spreads = {'L0_conv_V_b': (0.0, 0.798),
     'L0_conv_QK_b': (0.0, 0.8),
     'L0_conv_proj_b': (0.0, 0.341),
     'L0_conv_meta_b1': (0.0, 2.0),
     'L0_conv_meta_b2': (0.0, 2.0)}
    factors = {'L0_conv_V_w': 8.0,
     'L0_conv_QK_w': 8.0,
     'L0_conv_proj_w': 4.933,
     'L0_conv_meta_w1': 22.067,
     'L0_conv_meta_w2': 8.0,
     'L1_conv_merge_b': 4.473}
    for name, (base, spread) in spreads.items():
        noise = np.random.default_rng([zlib.crc32(name.encode()), seed]).standard_normal(out[name].shape)
        drawn = base * np.exp(spread * noise) if base else spread * noise
        out[name] = jnp.asarray(drawn.astype(out[name].dtype))
    for name, factor in factors.items():
        out[name] = (out[name] * factor).astype(out[name].dtype)
    return out
```

```python
from contextlib import ExitStack

import numpy as np

import concourse.bass as bass
from concourse import mybir

F32 = mybir.dt.float32
ALU = mybir.AluOpType
ACT = mybir.ActivationFunctionType
AX = mybir.AxisListType

C = 192
CA, CB = 128, 64
NH, HD, WS = 6, 32, 8
N = WS * WS
G, CG = 32, 6
EPS = 1e-5
NF = 94
HID = 256
ROWS = 4
STAT = 512
LOAD = 4096
NLOAD = 3


def fourier():
    n = np.arange(WS)
    rows, cols = np.meshgrid(n, n, indexing="ij")
    forward, inverse = [], []
    scale = HD ** -0.5 / N
    for u in range(WS):
        for v in range(WS):
            if (-u % WS, -v % WS) < (u, v):
                continue
            theta = (2 * np.pi / WS * ((u * rows + v * cols) % WS)).ravel()
            c, s = np.cos(theta), np.sin(theta)
            if (-u % WS, -v % WS) == (u, v):
                forward.append(np.round(c))
                inverse.append(scale * np.round(c))
            else:
                forward += [c, -s, c - s]
                inverse += [2 * scale * (c + s), 2 * scale * (s - c), -2 * scale * s]
    return np.array(forward).T, np.array(inverse)


def constants(B):
    forward, inverse = fourier()
    fwd = np.zeros((2, N, 2, NF))
    for w in range(2):
        fwd[w, :, w] = forward
    coords = np.stack(np.meshgrid(np.arange(WS), np.arange(WS), indexing="ij")).reshape(2, -1)
    rp = (coords[:, :, None] - coords[:, None, :]).astype(np.float32)
    rp = np.sign(rp) * np.log1p(np.abs(rp))
    channel, group = np.arange(C), np.arange(min(B * G, 128))
    return {
        "fwd": fwd.reshape(128, 2 * NF),
        "inv": inverse,
        "rp": rp.transpose(0, 2, 1).reshape(2, N * N),
        "ident": np.eye(128),
        "spread": group[:, None] % G == channel[None] // CG,
        "image": group[:, None] // G == np.arange(len(group) // G)[None],
        "mates": (channel[:, None] // CG == channel[None] // CG) / CG,
    }


def program(nc, x, out, w):
    B, _, H, W = x.shape
    assert W == 128 and H % 16 == 0
    NP = H * W // 128
    SPAIRS = W // 16
    UN = 2 * SPAIRS
    NB = NP // UN
    LAST = 3
    PW = W + 2
    NCH = H // ROWS
    CE = ROWS * W
    TG = min(B * G, 128)
    NT = B * G // TG
    NIMG = TG // G
    GS = CG * H * W
    NL = GS // LOAD
    assert NL % NLOAD == 0 and CE == STAT

    with ExitStack() as ctx:
        def sb(name, shape):
            return ctx.enter_context(nc.sbuf_tensor(name, shape, F32))

        def ps(name, banks):
            return ctx.enter_context(nc.psum_tensor(name, [128, 512 * banks], F32))

        def sem(name):
            return ctx.enter_context(nc.semaphore(name))

        plane = (H + 2) * PW
        x1 = sb("x1", [128, max(2 * plane, 3 * N * N + NLOAD * LOAD + GS // STAT * 6)])
        x1a = x1[:, 0:plane].rearrange("p (r c) -> p r c", c=PW)
        x1b = x1[0:CB, plane:2 * plane].rearrange("p (r c) -> p r c", c=PW)
        xs = sb("xs", [128, 2, 2, WS * W])
        wq = sb("wq", [128, 2, 3 * C])
        wn = sb("wn", [128, 2, 3 * C])
        wp = sb("wp", [128, 2, C])
        wm = sb("wm", [128, 2, C])
        mn = sb("mn", [128, 2, C])
        qkvb = sb("qkvb_row", [1, 3 * C])
        biases = sb("biases", [128, 3 * C])
        negmean = sb("negmean", [128, 2, 128])
        pb, mb, mc = sb("pb", [128, 2]), sb("mb", [128, 2]), sb("mc", [128, 2])
        fwd, inv = sb("fwd_sb", [128, 2, NF]), sb("inv_sb", [NF, N])
        ident, ones = sb("ident_sb", [128, 128]), sb("ones", [128, 128])
        spread, image = sb("spread_sb", [TG, C]), sb("image_sb", [TG, NIMG])
        mates = sb("mates_sb", [128, 2, C])
        mw1, mb1 = sb("mw1", [2, HID]), sb("mb1", [128, HID // 128])
        mw2, mb2 = sb("mw2", [128, HID // 128, NH]), sb("mb2", [1, N * NH])
        posb = sb("posb", [128, NH, N])
        gst, gsel = sb("gst", [TG, 8]), sb("gsel", [TG, 2, NIMG])
        st0 = sb("st0", [128, 2, 2, B])
        sm = sb("sm", [128, 8, 2])
        bn1 = sb("bn1", [128, 2, NCH, 6])
        xw = sb("xw", [128, 2, 4, 128])
        qk = sb("qk", [128, 2 * C])
        v = sb("v", [128, 4, 256])
        vbd = sb("vbd", [128, 4, 2, 3, 64])
        qh, prod = sb("qh", [NF, 2, C]), sb("prod", [NF, 2, C])
        vT, oT, yT = sb("vT", [128, 256]), sb("oT", [128, 256]), sb("yT", [128, 256])
        probs = sb("probs", [128, 2, NH, N])
        smax, ssum, srec = sb("smax", [128, 2, NH]), sb("ssum", [128, 2, NH]), sb("srec", [128, 2, NH])
        probsT = sb("probsT", [128, 3, 2, N])
        ud = sb("ud", [128, 2, CE])

        rp = x1[0:2, 0:N * N]
        hid = x1[:, N * N:3 * N * N].rearrange("p (t n) -> p t n", t=2)
        ld = x1[0:TG, 3 * N * N:3 * N * N + NLOAD * LOAD].rearrange("p (k n) -> p k n", k=NLOAD)
        bn0 = x1[0:TG, 3 * N * N + NLOAD * LOAD:][:, 0:GS // STAT * 6].rearrange("p (k n) -> p k n", n=6)

        def z(t, k):
            return xs[0:CA if t == 0 else CB, t, 0, k * CE:(k + 1) * CE]

        def res(t, k):
            return xs[0:CA if t == 0 else CB, t, 1, k * CE:(k + 1) * CE]

        b_qk, b_v, b_t, b_o, b_s, b_p = ps("b_qk", 1), ps("b_v", 1), ps("b_t", 2), ps("b_o", 1), ps("b_s", 2), ps("b_p", 1)

        const_in = sem("const_in")
        image_sent = sem("image_sent")
        ld_in = [sem(f"ld_in{k}") for k in range(NLOAD)]
        strip_in = [sem(f"strip_in{k}") for k in range(2)]
        out_sent = [sem(f"out_sent{k}") for k in range(2)]
        sbuf_zero, psum_zero, hid_mm, hid_relu, pos_mm = map(sem, ("sbuf_zero", "psum_zero", "hid_mm", "hid_relu", "pos_mm"))
        ld_read, gsel_done, spread_mm, spread_out = map(sem, ("ld_read", "gsel_done", "spread_mm", "spread_out"))
        dve_chain, var_done, sqrt_done = map(sem, ("dve_chain", "var_done", "sqrt_done"))
        norm0_w, bias_mm, bias_done = map(sem, ("norm0_w", "bias_mm", "bias_done"))
        mc_done, st_mean, st_dev, norm1_w, mean_mm, dev_mm, mbias_mm = map(sem, (
            "mc_done", "st_mean", "st_dev", "norm1_w", "mean_mm", "dev_mm", "mbias_mm"))
        xw_done, s_half, qk_mm, v_mm, t_mm, vT_mm, s_mm, pT_mm, y_mm, proj_mm, o_mm = map(sem, (
            "xw_done", "s_half", "qk_mm", "v_mm", "t_mm", "vT_mm", "s_mm", "pT_mm", "y_mm", "proj_mm", "o_mm"))
        qk_out, v_out, prod_done, s_out, max_done, sum_done, rec_done, x1_done = map(sem, (
            "qk_out", "v_out", "prod_done", "s_out", "max_done", "sum_done", "rec_done", "x1_done"))
        qh_out, vT_out, exp_done, pT_out, yT_out, oT_out, vbd_act, vbd_dve = map(sem, (
            "qh_out", "vT_out", "exp_done", "pT_out", "yT_out", "oT_out", "vbd_act", "vbd_dve"))
        sub_done, norm_done = map(sem, ("sub_done", "norm_done"))
        ud_done, lr_done, nb_done, z_done, merge_mm, resb_done, fin_a, fin_b = map(sem, (
            "ud_done", "lr_done", "nb_done", "z_done", "merge_mm", "resb_done", "fin_a", "fin_b"))

        loads = [
            (wq[:, 0], w["wqkvT"][0:CA]), (wq[0:CB, 1], w["wqkvT"][CA:C]),
            (wp[:, 0], w["projT"][0:CA]), (wp[0:CB, 1], w["projT"][CA:C]),
            (wm[:, 0], w["mergeT"][0:CA]), (wm[0:CB, 1], w["mergeT"][CA:C]),
            (mates[:, 0], w["mates"][0:CA]), (mates[0:CB, 1], w["mates"][CA:C]),
            (pb[:, 0:1], w["projb"][0:CA]), (pb[0:CB, 1:2], w["projb"][CA:C]),
            (mb[:, 0:1], w["mergeb"][0:CA]), (mb[0:CB, 1:2], w["mergeb"][CA:C]),
            (qkvb[:, :], w["qkvb"]), (fwd[:, :, :], w["fwd"].rearrange("p (w f) -> p w f", w=2)),
            (inv[:, :], w["inv"]), (ident[:, :], w["ident"]), (spread[:, :], w["spread"]),
            (image[:, :], w["image"]), (rp, w["rp"]), (mw1[:, :], w["w1"]), (mb1[:, :], w["b1"]),
            (mw2[:, :, :], w["w2"].rearrange("(t p) h -> p t h", p=128)), (mb2[:, :], w["b2"]),
        ]

        def pair_loop(eng, b, stages):
            for j in range(UN):
                stages(j, b * NP + j, 0, lambda lag, j=j: lag <= j)
            with eng.Fori(1, NB) as d:
                for j in range(UN):
                    stages(j, b * NP + d * UN + j, d * 2, lambda lag: True)
            for j in range(LAST):
                stages(j, b * NP + NP + j, 2 * NB, lambda lag, j=j: lag > j)

        def chunk_loop(eng, b, stages):
            for k in range(2):
                stages(k, b * NCH + k, k, True)
            with eng.Fori(1, NCH // 2) as d:
                for k in range(2):
                    stages(k, b * NCH + d * 2 + k, d * 2 + k, False)

        block = ctx.enter_context(nc.Block())

        @block.sync
        def _(sp):
            for dst, src in loads:
                sp.dma_start(dst, src).then_inc(const_in, 16)
            xg = x.rearrange("b (g c) h w -> (b g) (c h w)", g=G)
            for t in range(NT):
                for c in range(NL):
                    n = t * NL + c
                    if n >= NLOAD:
                        sp.wait_ge(ld_read, n - NLOAD + 1)
                    sp.dma_start(ld[:, n % NLOAD, :], xg[t * TG:(t + 1) * TG, c * LOAD:(c + 1) * LOAD]
                                 ).then_inc(ld_in[n % NLOAD], 16)

            def strip(b, s, k):
                rows = bass.ds(s * WS, WS)
                sp.dma_start(xs[:, 0, k, :].rearrange("p (r c) -> p r c", c=W), x[b, 0:CA, rows, :]
                             ).then_inc(strip_in[k], 16)
                sp.dma_start(xs[0:CB, 1, k, :].rearrange("p (r c) -> p r c", c=W), x[b, CA:C, rows, :]
                             ).then_inc(strip_in[k], 16)

            with sp.Fori(0, B) as b:
                for k in range(2):
                    strip(b, k, k)
                with sp.Fori(1, NB) as d:
                    for k in range(2):
                        sp.wait_ge(x1_done, b * NP + d * UN + ((k + 1) * SPAIRS - UN))
                        strip(b, d * 2 + k, k)

                def send(k, n, q, first):
                    rows = bass.ds(q * ROWS, ROWS)
                    sp.wait_ge(fin_a, n + 1)
                    sp.dma_start(out[b, 0:CA, rows, :], res(0, k).rearrange("p (r c) -> p r c", c=W)
                                 ).then_inc(out_sent[k], 16)
                    sp.wait_ge(fin_b, n + 1)
                    sp.dma_start(out[b, CA:C, rows, :], res(1, k).rearrange("p (r c) -> p r c", c=W)
                                 ).then_inc(out_sent[k], 16)

                chunk_loop(sp, b, send)
                for k in range(2):
                    sp.wait_ge(out_sent[k], b * (16 * NCH) + 16 * NCH)
                sp.sem_inc(image_sent, 1)

        @block.tensor
        def _(pe):
            mm = nc.tensor.matmul
            pe.wait_ge(const_in, 16 * len(loads))
            pe.wait_ge(sbuf_zero, 1)
            pe.wait_ge(psum_zero, 1)
            for k in range(N * N // 512):
                for t in range(2):
                    if k:
                        pe.wait_ge(hid_relu, 2 * k + t - 1)
                    mm(b_t[:, t * 512:(t + 1) * 512], mw1[:, t * 128:(t + 1) * 128],
                       rp[:, k * 512:(k + 1) * 512], start=True, stop=True).then_inc(hid_mm, 1)
            pe.wait_ge(hid_relu, 2 * (N * N // 512))
            for m in range(N):
                for t in range(2):
                    for half in range(2):
                        mm(b_qk[half * N:(half + 1) * N, m * NH:(m + 1) * NH], hid[:, t, m * N:(m + 1) * N],
                           mw2[:, t, :], start=(m == 0 and t == 0), stop=False, skip_group_check=True)
            mm(b_qk[:, 0:N * NH], ones[0:1, :], mb2[:, :], start=False, stop=True,
               skip_group_check=True).then_inc(pos_mm, 1)
            for t in range(NT):
                pe.wait_ge(gsel_done, t + 1)
                rhs = gsel[:, :, :].rearrange("p s i -> p (s i)")
                if t:
                    pe.wait_ge(spread_out, t)
                mm(b_v[:, 0:2 * NIMG], spread[:, 0:CA], rhs, start=True, stop=True)
                mm(b_v[0:CB, 64:64 + 2 * NIMG], spread[:, CA:C], rhs, start=True, stop=True).then_inc(spread_mm, 1)

            def scores(heads):
                for h in heads:
                    p, o, c = 32 * (h % 4), 128 * (h // 4), (h % 2) * 512 + (h // 2) * N
                    for win in range(2):
                        cols = slice(o + win * N, o + (win + 1) * N)
                        last = mm(b_s[win * N:(win + 1) * N, c:c + N], oT[p:p + HD, cols], vT[p:p + HD, cols],
                                  start=True, stop=True)
                return last

            with pe.Fori(0, B) as b:
                pe.wait_ge(norm0_w, b + 1)
                for o, lo, hi in ((b_qk, 0, 2 * C), (b_v, 2 * C, 3 * C)):
                    mm(o[:, 0:hi - lo], ones[0:1, :], qkvb[:, lo:hi], start=True, stop=False)
                    mm(o[:, 0:hi - lo], negmean[:, 0, :], wn[:, 0, lo:hi], start=False, stop=False)
                    last = mm(o[:, 0:hi - lo], negmean[0:CB, 1, :], wn[0:CB, 1, lo:hi], start=False, stop=True)
                last.then_inc(bias_mm, 1)
                pe.wait_ge(bias_done, b + 1)

                def stages(j, g, s, on):
                    if on(0):
                        pe.wait_ge(xw_done, g + 1)
                        xa, xb = xw[:, 0, j % 4, :], xw[0:CB, 1, j % 4, :]
                        mm(b_qk[:, 0:2 * C], xa, wn[:, 0, 0:2 * C], start=True, stop=False)
                        mm(b_qk[:, 0:2 * C], xb, wn[0:CB, 1, 0:2 * C], start=False, stop=True).then_inc(qk_mm, 1)
                        if on(1):
                            pe.wait_ge(vT_out, g)
                        mm(b_v[:, 0:C], xa, wn[:, 0, 2 * C:], start=True, stop=False)
                        mm(b_v[:, 0:C], xb, wn[0:CB, 1, 2 * C:], start=False, stop=True).then_inc(v_mm, 1)
                    if on(1):
                        pe.wait_ge(vT_out, g)
                        pe.wait_ge(oT_out, g)
                        if on(2):
                            pe.wait_ge(s_out, g - 1)
                        scores((0, 4, 1, 5)).then_inc(s_half, 1)
                    if on(2):
                        pe.wait_ge(norm_done, g - 1)
                        if on(3):
                            pe.wait_ge(yT_out, g - 2)
                        for t in range(3):
                            last = nc.tensor.transpose(
                                b_p[:, t * 128:(t + 1) * 128],
                                probs[:, j % 2, 2 * t:2 * t + 2, :].rearrange("p h m -> p (h m)"), ident[:, :])
                        last.then_inc(pT_mm, 1)
                    if on(1):
                        pe.wait_ge(s_half, g)
                        scores((2, 3)).then_inc(s_mm, 1)
                    if on(3):
                        pe.wait_ge(yT_out, g - 2)
                        if not on(1):
                            pe.wait_ge(x1_done, g - 3)
                        ya = yT[:, 0:128].rearrange("p (w r c) -> p r w c", w=2, c=WS)
                        yb = yT[0:CB, 128:256].rearrange("p (w r c) -> p r w c", w=2, c=WS)
                        mm(b_o[:, 0:128], wp[:, 0, 0:CA], ya, start=True, stop=False)
                        mm(b_o[:, 0:128], wp[0:CB, 1, 0:CA], yb, start=False, stop=True)
                        mm(b_o[0:CB, 128:256], wp[:, 0, CA:C], ya, start=True, stop=False)
                        mm(b_o[0:CB, 128:256], wp[0:CB, 1, CA:C], yb, start=False, stop=True).then_inc(proj_mm, 1)
                    if on(0):
                        pe.wait_ge(qk_out, g + 1)
                        for win in range(2):
                            mm(b_t[0:NF, win * 512:win * 512 + 2 * C], fwd[:, win, :], qk[:, :],
                               start=True, stop=True).then_inc(t_mm, 1)
                        pe.wait_ge(v_out, g + 1)
                        nc.tensor.transpose(b_v[:, 256:384], v[:, j % 4, 0:128], ident[:, :])
                        nc.tensor.transpose(b_v[:, 384:512], v[:, j % 4, 128:256], ident[:, :]).then_inc(vT_mm, 1)
                    if on(2):
                        pe.wait_ge(pT_out, g - 1)
                        pe.wait_ge(vbd_act, g - 1)
                        pe.wait_ge(vbd_dve, g - 1)
                        for t in range(3):
                            p, c = (t % 2) * 64, (t // 2) * 128
                            for win in range(2):
                                last = mm(b_p[p:p + 64, c + win * N:c + (win + 1) * N], vbd[:, (j - 2) % 4, win, t, :],
                                          probsT[:, t, win, :], start=True, stop=True)
                        last.then_inc(y_mm, 1)
                    if on(0):
                        if on(3):
                            pe.wait_ge(x1_done, g - 2)
                        for win in range(2):
                            pe.wait_ge(prod_done, g * 2 + win + 1)
                            mm(b_o[:, win * N:(win + 1) * N], prod[:, win, 0:CA], inv[:, :], start=True, stop=True)
                            last = mm(b_o[0:CB, 128 + win * N:128 + (win + 1) * N], prod[:, win, CA:C], inv[:, :],
                                      start=True, stop=True)
                        last.then_inc(o_mm, 1)

                pair_loop(pe, b, stages)

                def channels(weights, field, width):
                    rhs = sm[:, field:field + width, :]
                    mm(b_v[:, 0:width], weights[:, 0, 0:CA], rhs[:, :, 0], start=True, stop=False)
                    mm(b_v[:, 0:width], weights[0:CB, 1, 0:CA], rhs[0:CB, :, 1], start=False, stop=True)
                    mm(b_v[0:CB, 64:64 + width], weights[:, 0, CA:C], rhs[:, :, 0], start=True, stop=False)
                    return mm(b_v[0:CB, 64:64 + width], weights[0:CB, 1, CA:C], rhs[0:CB, :, 1], start=False, stop=True)

                pe.wait_ge(st_mean, b + 1)
                channels(mates, 0, 2).then_inc(mean_mm, 1)
                pe.wait_ge(st_dev, b + 1)
                channels(mates, 4, 1).then_inc(dev_mm, 1)
                pe.wait_ge(norm1_w, b + 1)
                channels(mn, 2, 1).then_inc(mbias_mm, 1)

                def merge(k, n, q, first):
                    pe.wait_ge(z_done, n + 1)
                    if not first:
                        pe.wait_ge(fin_a, n - 1)
                        pe.wait_ge(resb_done, n - 1)
                    for o, lo, hi in ((b_t[:, k * 512:k * 512 + CE], 0, CA), (b_s[0:CB, k * 512:k * 512 + CE], CA, C)):
                        mm(o, mn[:, 0, lo:hi], z(0, k), start=True, stop=False)
                        last = mm(o, mn[0:CB, 1, lo:hi], z(1, k), start=False, stop=True)
                    last.then_inc(merge_mm, 1)

                chunk_loop(pe, b, merge)

        @block.vector
        def _(dve):
            V = nc.vector
            V.memset(b_o[:, :], 0.0).then_inc(psum_zero, 1)
            chain = [0, 0]

            def link(ins):
                chain[1] += 1
                ins.then_inc(dve_chain, 1)
                dve.wait_ge(dve_chain, chain[0] + chain[1])

            def rstd(var, sd, r, t, wait):
                link(V.tensor_scalar(var, var, EPS, None, ALU.add))
                V.tensor_copy(t, var).then_inc(var_done, 1)
                dve.wait_ge(sqrt_done, wait)
                link(V.reciprocal(r, sd))
                link(V.tensor_tensor(t, var, r, ALU.mult))
                link(V.tensor_tensor(t, t, r, ALU.mult))
                link(V.tensor_scalar(t, t, -0.5, 1.5, ALU.mult, ALU.add))
                link(V.tensor_tensor(r, r, t, ALU.mult))

            dve.wait_ge(const_in, 16 * len(loads))
            dve.wait_ge(sbuf_zero, 1)
            for t in range(NT):
                for c in range(NL):
                    n = t * NL + c
                    dve.wait_ge(ld_in[n % NLOAD], 16 * (n // NLOAD + 1))
                    for i in range(LOAD // STAT):
                        last = V.bn_stats(bn0[:, c * (LOAD // STAT) + i, :], ld[:, n % NLOAD, i * STAT:(i + 1) * STAT])
                    last.then_inc(ld_read, 1)
                dve.wait_ge(ld_read, (t + 1) * NL)
                link(V.bn_aggr(gst[:, 0:2], bn0[:, :, :].rearrange("p k n -> p (k n)")))
                rstd(gst[:, 1:2], gst[:, 2:3], gst[:, 3:4], gst[:, 4:5], t + 1)
                V.tensor_scalar(gsel[:, 0, :], image[:, :], gst[:, 0:1], None, ALU.mult)
                V.tensor_scalar(gsel[:, 1, :], image[:, :], gst[:, 3:4], None, ALU.mult).then_inc(gsel_done, 1)
                dve.wait_ge(spread_mm, t + 1)
                to = st0[:, :, :, t * NIMG:(t + 1) * NIMG]
                V.tensor_copy(to[:, 0], b_v[:, 0:2 * NIMG].rearrange("p (s i) -> p s i", s=2))
                link(V.tensor_copy(to[0:CB, 1], b_v[0:CB, 64:64 + 2 * NIMG].rearrange("p (s i) -> p s i", s=2)))
                if t + 1 < NT:
                    V.tensor_copy(gst[:, 7:8], gst[:, 0:1]).then_inc(spread_out, 1)
            dve.wait_ge(pos_mm, 1)
            link(V.tensor_copy(posb[:, :, :], b_qk[:, 0:N * NH].rearrange("p (m h) -> p h m", h=NH)))
            chained = chain[1]

            with dve.Fori(0, B) as b:
                PER_IMAGE = 13
                chain[0], chain[1] = b * PER_IMAGE, chained
                for t, n in ((0, CA), (1, CB)):
                    V.tensor_scalar(wn[0:n, t, :], wq[0:n, t, :], st0[0:n, t, 1, bass.ds(b, 1)], None, ALU.mult)
                for t, n in ((0, CA), (1, CB)):
                    last = V.tensor_scalar(negmean[0:n, t, :], ones[0:n, :], st0[0:n, t, 0, bass.ds(b, 1)], -1.0,
                                           ALU.mult, ALU.mult)
                last.then_inc(norm0_w, 1)
                dve.wait_ge(bias_mm, b + 1)
                V.tensor_copy(biases[:, 0:2 * C], b_qk[:, 0:2 * C])
                V.tensor_copy(biases[:, 2 * C:], b_v[:, 0:C]).then_inc(bias_done, 1)
                dve.wait_ge(bias_done, b + 1)

                def stages(j, g, s, on):
                    if on(0):
                        dve.wait_ge(qk_mm, g + 1)
                        V.tensor_tensor(qk[:, :], b_qk[:, 0:2 * C], biases[:, 0:2 * C], ALU.add).then_inc(qk_out, 1)
                        dve.wait_ge(v_mm, g + 1)
                        V.tensor_tensor(v[:, j % 4, 0:C], b_v[:, 0:C], biases[:, 2 * C:], ALU.add).then_inc(v_out, 1)
                    if on(1):
                        pr = probs[:, (j - 1) % 2, :, :]
                        order = "p (i h) m -> p h i m"
                        dve.wait_ge(s_mm, g)
                        V.tensor_tensor(pr.rearrange(order, h=2),
                                        b_s[:, :].rearrange("p (h c) -> p h c", h=2)[:, :, 0:3 * N]
                                        .rearrange("p h (i m) -> p h i m", m=N),
                                        posb[:, :, :].rearrange(order, h=2), ALU.add).then_inc(s_out, 1)
                        dve.wait_ge(s_out, g)
                        V.tensor_reduce(smax[:, (j - 1) % 2, :], pr, AX.X, ALU.max).then_inc(max_done, 1)
                    if on(3):
                        i = j - 3
                        row, col, k = (s + i // SPAIRS) * WS + 1, (i % SPAIRS) * 16, (i % UN) // SPAIRS
                        dve.wait_ge(proj_mm, g - 2)
                        for t, n, xt in ((0, CA, x1a), (1, CB, x1b)):
                            last = V.scalar_tensor_tensor(
                                out=xt[:, bass.ds(row, WS), col + 1:col + 17],
                                in0=b_o[0:n, t * 128:(t + 1) * 128].rearrange("p (r c) -> p r c", c=16),
                                scalar=pb[0:n, t:t + 1],
                                in1=xs[0:n, t, k, :].rearrange("p (r c) -> p r c", c=W)[:, :, col:col + 16],
                                op0=ALU.add, op1=ALU.add)
                        last.then_inc(x1_done, 1)
                    if on(0):
                        for win in range(2):
                            dve.wait_ge(qh_out, g * 2 + win + 1)
                            V.tensor_tensor(prod[:, win, :], qh[:, win, :], b_t[0:NF, win * 512 + C:win * 512 + 2 * C],
                                            ALU.mult).then_inc(prod_done, 1)
                        vv = v[:, j % 4, 0:C].rearrange("p (t h d) -> p t h d", h=2, d=HD)
                        dve.wait_ge(v_out, g + 1)
                        V.tensor_copy(vbd[0:64, j % 4, 0, :, 0:HD], vv[0:64, :, 0, :])
                        V.tensor_copy(vbd[64:128, j % 4, 1, :, HD:], vv[64:128, :, 1, :]).then_inc(vbd_dve, 1)
                    if on(3) and (j - 3) % SPAIRS == SPAIRS - 1:
                        dve.wait_ge(x1_done, g - 2)
                        for t, n, xt in ((0, CA, x1a), (1, CB, x1b)):
                            for half in range(2):
                                V.bn_stats(bn1[0:n, t, bass.ds((s + i // SPAIRS) * 2 + half, 1), :],
                                           xt[:, bass.ds(row + half * ROWS, ROWS), 1:W + 1])
                    if on(1):
                        dve.wait_ge(exp_done, g)
                        V.tensor_reduce(ssum[:, (j - 1) % 2, :], probs[:, (j - 1) % 2, :, :], AX.X, ALU.add
                                        ).then_inc(sum_done, 1)
                        dve.wait_ge(sum_done, g)
                        V.reciprocal(srec[:, (j - 1) % 2, :], ssum[:, (j - 1) % 2, :]).then_inc(rec_done, 1)

                pair_loop(dve, b, stages)

                link(V.memset(sm[:, 7, :], 0.0))
                V.memset(sm[:, 6, :], 0.0)
                for t, n in ((0, CA), (1, CB)):
                    last = V.bn_aggr(sm[0:n, 0:2, t], bn1[0:n, t, :, :].rearrange("p k n -> p (k n)"))
                last.then_inc(st_mean, 1)
                dve.wait_ge(mean_mm, b + 1)
                V.tensor_copy(sm[:, 2:4, 0], b_v[:, 0:2])
                link(V.tensor_copy(sm[0:CB, 2:4, 1], b_v[0:CB, 64:66]))
                link(V.tensor_tensor(sm[:, 4, :], sm[:, 0, :], sm[:, 2, :], ALU.subtract))
                V.tensor_tensor(sm[:, 4, :], sm[:, 4, :], sm[:, 4, :], ALU.mult).then_inc(st_dev, 1)
                dve.wait_ge(dev_mm, b + 1)
                link(V.tensor_tensor(sm[:, 5, 0:1], b_v[:, 0:1], sm[:, 3, 0:1], ALU.add))
                link(V.tensor_tensor(sm[0:CB, 5, 1:2], b_v[0:CB, 64:65], sm[0:CB, 3, 1:2], ALU.add))
                rstd(sm[:, 5, :], sm[:, 6, :], sm[:, 7, :], sm[:, 4, :], b + NT + 1)
                for t, n, xt in ((0, CA, x1a), (1, CB, x1b)):
                    last = V.tensor_scalar(mn[0:n, t, :], wm[0:n, t, :], sm[0:n, 7, t:t + 1], None, ALU.mult)
                    for edge in (0, PW - 1):
                        V.tensor_scalar(xt[:, :, edge], ones[0:n, 0:1].broadcast_to([n, H + 2]), sm[0:n, 2, t:t + 1],
                                        None, ALU.mult)
                    for edge in (0, H + 1):
                        last = V.tensor_scalar(xt[:, edge, 1:PW - 1], ones[0:n, 0:1].broadcast_to([n, W]),
                                               sm[0:n, 2, t:t + 1], None, ALU.mult)
                last.then_inc(norm1_w, 1)
                dve.wait_ge(mbias_mm, b + 1)
                link(V.tensor_tensor(mc[:, 0:1], mb[:, 0:1], b_v[:, 0:1], ALU.subtract))
                link(V.tensor_tensor(mc[0:CB, 1:2], mb[0:CB, 1:2], b_v[0:CB, 64:65], ALU.subtract))
                V.tensor_copy(sm[:, 4, :], mc[:, :]).then_inc(mc_done, 1)

                assert chain[1] - chained == PER_IMAGE

                def stencil(k, n, q, first):
                    rows = bass.ds(q * ROWS + 1, ROWS)
                    zz = [z(t, k).rearrange("p (r c) -> p r c", c=W) for t in range(2)]
                    for t, xt in ((0, x1a), (1, x1b)):
                        V.tensor_tensor(zz[t], xt[:, rows, 0:W], xt[:, rows, 2:W + 2], ALU.add).then_inc(lr_done, 1)
                    dve.wait_ge(ud_done, n + 1)
                    dve.wait_ge(lr_done, n * 2 + 2)
                    for t in range(2):
                        last = V.tensor_tensor(z(t, k), z(t, k), ud[0:CA if t == 0 else CB, t, :], ALU.add)
                    last.then_inc(nb_done, 1)
                    dve.wait_ge(nb_done, n + 1)
                    for t, xt in ((0, x1a), (1, x1b)):
                        last = V.scalar_tensor_tensor(out=zz[t], in0=xt[:, rows, 1:W + 1], scalar=5.0, in1=zz[t],
                                                      op0=ALU.mult, op1=ALU.subtract)
                    last.then_inc(z_done, 1)

                def result(k, n, q, first):
                    dve.wait_ge(merge_mm, n + 1)
                    if not first:
                        dve.wait_ge(out_sent[k], n * 16 - k * 16)
                    V.scalar_tensor_tensor(
                        out=res(0, k).rearrange("p (r c) -> p r c", c=W),
                        in0=b_t[:, k * 512:k * 512 + CE].rearrange("p (r c) -> p r c", c=W), scalar=mc[:, 0:1],
                        in1=x1a[:, bass.ds(q * ROWS + 1, ROWS), 1:W + 1], op0=ALU.add, op1=ALU.add).then_inc(fin_a, 1)

                n0 = b * NCH
                stencil(0, n0, 0, True)
                stencil(1, n0 + 1, 1, True)
                result(0, n0, 0, True)
                with dve.Fori(1, NCH // 2) as d:
                    n, q = b * NCH + d * 2, d * 2
                    stencil(0, n, q, False)
                    result(1, n - 1, q - 1, None)
                    stencil(1, n + 1, q + 1, False)
                    result(0, n, q, False)
                result(1, n0 + NCH - 1, NCH - 1, False)
                dve.wait_ge(fin_b, n0 + NCH)

        @block.scalar
        def _(act):
            A = nc.scalar

            def copy(o, i):
                return A.activation(o, i, ACT.Copy)

            for k in range(N * N // 512):
                for t in range(2):
                    act.wait_ge(hid_mm, 2 * k + t + 1)
                    A.activation(hid[:, t, k * 512:(k + 1) * 512], b_t[:, t * 512:(t + 1) * 512], ACT.Relu,
                                 bias=mb1[:, t:t + 1]).then_inc(hid_relu, 1)
            for t in range(NT):
                act.wait_ge(var_done, t + 1)
                A.activation(gst[:, 2:3], gst[:, 1:2], ACT.Sqrt).then_inc(sqrt_done, 1)

            with act.Fori(0, B) as b:
                def order_and_stages(j, g, s, on):
                    if on(0):
                        k, c = j // SPAIRS, (j % SPAIRS) * 2
                        if j % SPAIRS == 0:
                            act.wait_ge(strip_in[k], b * (NB * 32) + s * 16 + 32)
                        if on(4):
                            act.wait_ge(v_mm, g - 3)
                        for t, n in ((0, CA), (1, CB)):
                            last = copy(xw[0:n, t, j % 4, :].rearrange("p (w r c) -> p w r c", w=2, c=WS),
                                        xs[0:n, t, k, :].rearrange("p (r w c) -> p w r c", r=WS, c=WS)[:, c:c + 2])
                        last.then_inc(xw_done, 1)
                    stages(j - 1, g - 1, s, lambda lag: on(lag + 1))

                def stages(j, g, s, on):
                    if on(2):
                        act.wait_ge(pT_mm, g - 1)
                        copy(probsT[:, :, :, :].rearrange("p t w n -> p (t w n)"), b_p[:, 0:NH * N]).then_inc(pT_out, 1)
                    if on(0):
                        for win in range(2):
                            act.wait_ge(t_mm, g * 2 + win + 1)
                            copy(qh[:, win, :], b_t[0:NF, win * 512:win * 512 + C]).then_inc(qh_out, 1)
                        act.wait_ge(vT_mm, g + 1)
                        copy(vT[:, :], b_v[:, 256:512]).then_inc(vT_out, 1)
                    if on(1):
                        act.wait_ge(sub_done, g)
                        pr = probs[:, (j - 1) % 2, :, :].rearrange("p h m -> p (h m)")
                        A.activation(pr, pr, ACT.Exp).then_inc(exp_done, 1)
                    if on(2):
                        act.wait_ge(y_mm, g - 1)
                        copy(yT[:, :], b_p[:, 0:256]).then_inc(yT_out, 1)
                    if on(0):
                        act.wait_ge(o_mm, g + 1)
                        copy(oT[:, :], b_o[:, 0:256]).then_inc(oT_out, 1)
                        vv = v[:, j % 4, 0:C].rearrange("p (t h d) -> p t h d", h=2, d=HD)
                        copy(vbd[64:128, j % 4, 0, :, HD:], vv[0:64, :, 1, :])
                        copy(vbd[0:64, j % 4, 1, :, 0:HD], vv[64:128, :, 0, :]).then_inc(vbd_act, 1)

                pair_loop(act, b, order_and_stages)
                act.wait_ge(var_done, b + NT + 1)
                A.activation(sm[:, 6, :], sm[:, 5, :], ACT.Sqrt).then_inc(sqrt_done, 1)

                def result(k, n, q, first):
                    act.wait_ge(merge_mm, n + 1)
                    if not first:
                        act.wait_ge(out_sent[k], n * 16 - k * 16)
                    A.activation(res(1, k), b_s[0:CB, k * 512:k * 512 + CE], ACT.Identity,
                                 bias=mc[0:CB, 1:2]).then_inc(resb_done, 1)

                act.wait_ge(mc_done, b + 1)
                chunk_loop(act, b, result)

        @block.gpsimd
        def _(pool):
            P = nc.gpsimd
            pool.wait_ge(const_in, 16 * len(loads))
            P.memset(ones[:, :], 1.0)
            P.memset(v[:, :, :], 0.0)
            P.memset(mc[:, :], 0.0)
            P.memset(sm[:, :, :], 0.0)
            P.memset(vbd[:, :, :, :, :], 0.0).then_inc(sbuf_zero, 1)
            with pool.Fori(0, B) as b:
                def stages(j, g, s, on):
                    if on(1):
                        pr = probs[:, (j - 1) % 2, :, :]
                        pool.wait_ge(max_done, g)
                        P.tensor_tensor(pr, pr, smax[:, (j - 1) % 2, :].unsqueeze(2).broadcast_to([128, NH, N]),
                                        ALU.subtract).then_inc(sub_done, 1)
                    if on(1):
                        pool.wait_ge(rec_done, g)
                        P.tensor_tensor(pr, pr, srec[:, (j - 1) % 2, :].unsqueeze(2).broadcast_to([128, NH, N]),
                                        ALU.mult).then_inc(norm_done, 1)

                pair_loop(pool, b, stages)
                pool.wait_ge(norm1_w, b + 1)

                def updown(k, n, q, first):
                    if not first or k:
                        pool.wait_ge(nb_done, n)
                    for t, m, xt in ((0, CA, x1a), (1, CB, x1b)):
                        last = P.tensor_tensor(ud[0:m, t, :].rearrange("p (r c) -> p r c", c=W),
                                               xt[:, bass.ds(q * ROWS, ROWS), 1:W + 1],
                                               xt[:, bass.ds(q * ROWS + 2, ROWS), 1:W + 1], ALU.add)
                    last.then_inc(ud_done, 1)

                def result(k, n, q):
                    pool.wait_ge(resb_done, n + 1)
                    r = res(1, k).rearrange("p (r c) -> p r c", c=W)
                    P.tensor_tensor(r, r, x1b[:, bass.ds(q * ROWS + 1, ROWS), 1:W + 1], ALU.add).then_inc(fin_b, 1)

                n0 = b * NCH
                updown(0, n0, 0, True)
                updown(1, n0 + 1, 1, True)
                result(0, n0, 0)
                with pool.Fori(1, NCH // 2) as d:
                    n, q = b * NCH + d * 2, d * 2
                    updown(0, n, q, False)
                    result(1, n - 1, q - 1)
                    updown(1, n + 1, q + 1, False)
                    result(0, n, q)
                result(1, n0 + NCH - 1, NCH - 1)


def kernel(**inputs):
    import concourse.bacc as bacc
    from concourse.bass_utils import run_bass_kernel_spmd

    a = {k: np.asarray(v) for k, v in inputs.items()}
    x = a["x"]
    arrays = {
        "x": x,
        "wqkvT": np.ascontiguousarray(np.concatenate([a["L0_conv_QK_w"], a["L0_conv_V_w"]]).T),
        "qkvb": np.concatenate([a["L0_conv_QK_b"], a["L0_conv_V_b"]])[None],
        "projT": np.ascontiguousarray(a["L0_conv_proj_w"].T),
        "projb": a["L0_conv_proj_b"][:, None],
        "mergeT": np.ascontiguousarray(a["L1_conv_merge_w"][:, :, 0, 0].T),
        "mergeb": a["L1_conv_merge_b"][:, None],
        "w1": a["L0_conv_meta_w1"],
        "b1": np.ascontiguousarray(a["L0_conv_meta_b1"].reshape(-1, 128).T),
        "w2": a["L0_conv_meta_w2"],
        "b2": np.tile(a["L0_conv_meta_b2"], N)[None],
    }
    for name, value in constants(x.shape[0]).items():
        arrays[name] = np.ascontiguousarray(value, dtype=np.float32)
    nc = bacc.Bacc("TRN2", target_bir_lowering=False, num_devices=1)
    w = {name: nc.dram_tensor("in_" + name, value.shape, F32, kind="ExternalInput").ap()
         for name, value in arrays.items()}
    out = nc.dram_tensor("out", x.shape, F32, kind="ExternalOutput").ap()
    program(nc, w["x"], out, w)
    r = run_bass_kernel_spmd(nc, [{"in_" + name: value for name, value in arrays.items()}], core_ids=[0])
    return r.results[0]["out"]
```

```python
from contextlib import ExitStack

import numpy as np

import concourse.bass as bass
from concourse import mybir

F32 = mybir.dt.float32
F32R = mybir.dt.float32r
ALU = mybir.AluOpType
ACT = mybir.ActivationFunctionType
AX = mybir.AxisListType

C = 192
CA, CB = 128, 64
NH, HD, WS = 6, 32, 8
N = WS * WS
G, CG = 32, 6
EPS = 1e-5
NF = 94
HID = 256
ROWS = 4
STAT = 512
LOAD = 4096
HALF = 3 * C // 2
BIAS_ROWS = (64, 96)
NLOAD = 3


def fourier():
    n = np.arange(WS)
    rows, cols = np.meshgrid(n, n, indexing="ij")
    forward, inverse = [], []
    scale = HD ** -0.5 / N
    for u in range(WS):
        for v in range(WS):
            if (-u % WS, -v % WS) < (u, v):
                continue
            theta = (2 * np.pi / WS * ((u * rows + v * cols) % WS)).ravel()
            c, s = np.cos(theta), np.sin(theta)
            if (-u % WS, -v % WS) == (u, v):
                forward.append(np.round(c))
                inverse.append(scale * np.round(c))
            else:
                forward += [c, -s, c - s]
                inverse += [2 * scale * (c + s), 2 * scale * (s - c), -2 * scale * s]
    return np.array(forward).T, np.array(inverse)


def constants(B):
    forward, inverse = fourier()
    coords = np.stack(np.meshgrid(np.arange(WS), np.arange(WS), indexing="ij")).reshape(2, -1)
    rp = (coords[:, :, None] - coords[:, None, :]).astype(np.float32)
    rp = np.sign(rp) * np.log1p(np.abs(rp))
    channel, group = np.arange(C), np.arange(min(B * G, 128))
    return {
        "fwd": np.tile(forward, (2, 1)),
        "inv": inverse,
        "rp": rp.transpose(0, 2, 1).reshape(2, N * N),
        "ident": np.eye(128),
        "spread": group[:, None] % G == np.concatenate([channel, channel[CA:]])[None] // CG,
        "image": group[:, None] // G == np.arange(len(group) // G)[None],
        "mates": (channel[:, None] // CG == channel[None] // CG) / CG,
    }


def program(nc, x, out, w):
    B, _, H, W = x.shape
    assert W == 128 and H % 16 == 0
    NP = H * W // 128
    SPAIRS = W // 16
    UN = 2 * SPAIRS
    NB = NP // UN
    LAST = 4
    PW = W + 2
    NCH = H // ROWS
    CE = ROWS * W
    TG = min(B * G, 128)
    NT = B * G // TG
    NIMG = TG // G
    GS = CG * H * W
    NL = GS // LOAD
    assert NL % NLOAD == 0 and CE == STAT

    with ExitStack() as ctx:
        def sb(name, shape, dtype=F32):
            return ctx.enter_context(nc.sbuf_tensor(name, shape, dtype))

        def ps(name, banks):
            return ctx.enter_context(nc.psum_tensor(name, [128, 512 * banks], F32))

        def sem(name):
            return ctx.enter_context(nc.semaphore(name))

        plane = (H + 2) * PW
        x1 = sb("x1", [128, max(2 * plane, 3 * N * N + NLOAD * LOAD + GS // STAT * 6 + 768)])
        x1a = x1[:, 0:plane].rearrange("p (r c) -> p r c", c=PW)
        x1b = x1[0:CB, plane:2 * plane].rearrange("p (r c) -> p r c", c=PW)
        xs = sb("xs", [128, 2, 2, WS * W])
        wq = sb("wq", [128, 2, 3 * C])
        wnh, wnl = sb("wnh", [128, 2, 3 * C], F32R), sb("wnl", [128, 2, 3 * C], F32R)
        wp = sb("wp", [128, 2, C])
        wm = sb("wm", [128, 2, C])
        mn = sb("mn", [128, 2, C])
        qkvb = sb("qkvb_row", [1, 3 * C])
        shared = sb("shared", [128, 2624])
        at = [0]

        def share(*dims):
            n = int(np.prod(dims))
            at[0] += n
            a = shared[:, at[0] - n:at[0]]
            if len(dims) == 1:
                return a
            names = "abcd"[:len(dims)]
            return a.rearrange(f"p ({' '.join(names)}) -> p {' '.join(names)}", **dict(zip(names, dims)))

        probs = share(2, NH, N)
        probsT = share(3, 2, N)
        qh, prod = share(2, C)[0:NF], share(3, 2, 2, HD)[0:NF]
        bn1 = share(2, NCH, 6)
        wn = shared[:, 0:6 * C].rearrange("p (t n) -> p t n", t=2)
        negmean = shared[:, 6 * C:6 * C + 256].rearrange("p (t n) -> p t n", t=2)
        biasrow = shared[:, 6 * C + 256:9 * C + 256]
        assert max(at[0], 9 * C + 256) <= 2624
        diag = shared[:, 0:4 * (ROWS + 1) * (W + 1)].rearrange("p (t k r c) -> p t k r c", t=2, k=2, c=W + 1)
        pb, mb, mc = sb("pb", [128, 2]), sb("mb", [128, 2]), sb("mc", [128, 2])
        fwdh, fwdl = sb("fwdh", [128, NF], F32R), sb("fwdl", [128, NF], F32R)
        inv = sb("inv_sb", [NF, N])
        ident, ones = sb("ident_sb", [128, 128]), sb("ones", [128, 128])
        spread, image = sb("spread_sb", [TG, 256]), sb("image_sb", [TG, NIMG])
        mates = sb("mates_sb", [128, 2, C])
        posb = sb("posb", [128, NH, N])
        gst, gsel = sb("gst", [TG, 8]), sb("gsel", [TG, 2, NIMG])
        st0 = sb("st0", [128, 2, 2, B])
        sm = sb("sm", [128, 8, 2])
        xh, xl, xhl = (sb(name, [128, 2, 128], F32R) for name in ("xh", "xl", "xhl"))
        xhb = sb("xhb", [128, 2, 128], F32R)
        vt = sb("vt", [N, 2, 3, 2, 2, HD])
        vbd = sb("vbd", [128, 4, 2, 3, 64])
        vT = sb("vT", [128, 3, 2, N])
        obd = sb("obd", [128, 3, 2, N])
        yT = sb("yT", [128, 256])
        qk = sb("qk", [128, 2, 2 * C], F32R)
        smax, ssum, srec = sb("smax", [128, 2, NH]), sb("ssum", [128, 2, NH]), sb("srec", [128, 2, NH])

        rp = x1[0:2, 0:N * N]
        tail = 3 * N * N + NLOAD * LOAD + GS // STAT * 6
        fwd, mb1 = x1[:, tail:tail + NF], x1[:, tail + NF:tail + NF + 2]
        mw2 = x1[:, tail + NF + 2:][:, 0:2 * NH].rearrange("p (t h) -> p t h", t=2)
        mw1, mb2 = x1[0:2, tail + 128:tail + 128 + HID], x1[0:1, tail + 128 + HID:tail + 128 + HID + N * NH]
        hid = x1[:, N * N:3 * N * N].rearrange("p (t n) -> p t n", t=2)
        ld = x1[0:TG, 3 * N * N:3 * N * N + NLOAD * LOAD].rearrange("p (k n) -> p k n", k=NLOAD)
        bn0 = x1[0:TG, 3 * N * N + NLOAD * LOAD:][:, 0:GS // STAT * 6].rearrange("p (k n) -> p k n", n=6)

        def z(t, k):
            return xs[0:CA if t == 0 else CB, t, 0, k * CE:(k + 1) * CE]

        def res(t, k):
            return xs[0:CA if t == 0 else CB, t, 1, k * CE:(k + 1) * CE]

        b_q, b_t, b_o, b_s, b_p = ps("b_q", 2), ps("b_t", 2), ps("b_o", 1), ps("b_s", 2), ps("b_p", 1)
        half = [b_q[:, 0:HALF], b_q[:, 512:512 + HALF]]
        b_v = b_q[:, 512:1024]
        b_r = b_s[:, 512:1024]

        const_in = sem("const_in")
        image_sent = sem("image_sent")
        ld_in = [sem(f"ld_in{k}") for k in range(NLOAD)]
        strip_in = [sem(f"strip_in{k}") for k in range(2)]
        out_sent = [sem(f"out_sent{k}") for k in range(2)]
        sbuf_zero, psum_zero, hid_mm, hid_relu, pos_mm = map(sem, ("sbuf_zero", "psum_zero", "hid_mm", "hid_relu", "pos_mm"))
        ld_read, gsel_done, spread_mm, spread_out = map(sem, ("ld_read", "gsel_done", "spread_mm", "spread_out"))
        dve_chain, var_done, sqrt_done = map(sem, ("dve_chain", "var_done", "sqrt_done"))
        norm0_w, bias_mm, bias_done = map(sem, ("norm0_w", "bias_mm", "bias_done"))
        mc_done, st_mean, st_dev, norm1_w, mean_mm, dev_mm, mbias_mm = map(sem, (
            "mc_done", "st_mean", "st_dev", "norm1_w", "mean_mm", "dev_mm", "mbias_mm"))
        qkv_mm, t_mm, vT_mm, s_mm, pT_mm, y_mm, proj_mm, o_mm = map(sem, (
            "qkv_mm", "t_mm", "vT_mm", "s_mm", "pT_mm", "y_mm", "proj_mm", "o_mm"))
        v1_out, v_out, lo_out, prod_done, s_out, max_done, sum_done, rec_done, x1_done = map(sem, (
            "v1_out", "v_out", "lo_out", "prod_done", "s_out", "max_done", "sum_done", "rec_done", "x1_done"))
        hi_out, xh_done, xl_done, xhl_done, qh_out, vT_out, exp_done, pT_out, yT_out, oT_out, vbd_act, vbd_dve = map(sem, (
            "hi_out", "xh_done", "xl_done", "xhl_done", "qh_out", "vT_out", "exp_done", "pT_out", "yT_out", "oT_out", "vbd_act", "vbd_dve"))
        sub_done, norm_done = map(sem, ("sub_done", "norm_done"))
        diag_done, nb_done, z_done, merge_mm, fin_a, fin_b = map(sem, (
            "diag_done", "nb_done", "z_done", "merge_mm", "fin_a", "fin_b"))

        loads = [
            (wq[:, 0], w["wqkvT"][0:CA]), (wq[0:CB, 1], w["wqkvT"][CA:C]),
            (wq[CB:128, 1], w["wqkvT"][CA:C]),
            (wp[:, 0], w["projT"][0:CA]), (wp[0:CB, 1], w["projT"][CA:C]),
            (wm[:, 0], w["mergeT"][0:CA]), (wm[0:CB, 1], w["mergeT"][CA:C]),
            (mates[:, 0], w["mates"][0:CA]), (mates[0:CB, 1], w["mates"][CA:C]),
            (pb[:, 0:1], w["projb"][0:CA]), (pb[0:CB, 1:2], w["projb"][CA:C]),
            (mb[:, 0:1], w["mergeb"][0:CA]), (mb[0:CB, 1:2], w["mergeb"][CA:C]),
            (qkvb[:, :], w["qkvb"]), (fwd, w["fwd"]),
            (inv[:, :], w["inv"]), (ident[:, :], w["ident"]), (spread[:, :], w["spread"]),
            (image[:, :], w["image"]), (rp, w["rp"]), (mw1, w["w1"]), (mb1, w["b1"]),
            (mw2, w["w2"].rearrange("(t p) h -> p t h", p=128)), (mb2, w["b2"]),
        ]

        def pair_loop(eng, b, stages, last=LAST):
            for j in range(UN):
                stages(j, b * NP + j, 0, lambda lag, j=j: lag <= j)
            with eng.Fori(1, NB) as d:
                for j in range(UN):
                    stages(j, b * NP + d * UN + j, d * 2, lambda lag: True)
            for j in range(last):
                stages(j, b * NP + NP + j, 2 * NB, lambda lag, j=j: lag > j)

        def ahead(early, first, late):
            def all_three(j, g, s, on):
                early(j - 1, g - 1, s, lambda lag: on(lag + 1))
                if on(0):
                    first(j, g, s, on)
                late(j - 1, g - 1, s, lambda lag: on(lag + 1))
            return all_three

        def chunk_loop(eng, b, stages):
            for k in range(2):
                stages(k, b * NCH + k, k, True)
            with eng.Fori(1, NCH // 2) as d:
                for k in range(2):
                    stages(k, b * NCH + d * 2 + k, d * 2 + k, False)

        def pixels(t, k, c):
            return xs[0:CA if t == 0 else CB, t, k, :].rearrange("p (r w c) -> p w r c", r=WS, c=WS)[:, c:c + 2]

        block = ctx.enter_context(nc.Block())

        @block.sync
        def _(sp):
            for dst, src in loads:
                sp.dma_start(dst, src).then_inc(const_in, 16)
            xg = x.rearrange("b (g c) h w -> (b g) (c h w)", g=G)
            for t in range(NT):
                for c in range(NL):
                    n = t * NL + c
                    if n >= NLOAD:
                        sp.wait_ge(ld_read, n - NLOAD + 1)
                    sp.dma_start(ld[:, n % NLOAD, :], xg[t * TG:(t + 1) * TG, c * LOAD:(c + 1) * LOAD]
                                 ).then_inc(ld_in[n % NLOAD], 16)

            def strip(b, s, k):
                rows = bass.ds(s * WS, WS)
                sp.dma_start(xs[:, 0, k, :].rearrange("p (r c) -> p r c", c=W), x[b, 0:CA, rows, :]
                             ).then_inc(strip_in[k], 16)
                sp.dma_start(xs[0:CB, 1, k, :].rearrange("p (r c) -> p r c", c=W), x[b, CA:C, rows, :]
                             ).then_inc(strip_in[k], 16)

            with sp.Fori(0, B) as b:
                for k in range(2):
                    strip(b, k, k)
                with sp.Fori(1, NB) as d:
                    for k in range(2):
                        sp.wait_ge(x1_done, b * NP + d * UN + ((k + 1) * SPAIRS - UN))
                        strip(b, d * 2 + k, k)

                def send(k, n, q, first):
                    rows = bass.ds(q * ROWS, ROWS)
                    sp.wait_ge(fin_a, n + 1)
                    sp.dma_start(out[b, 0:CA, rows, :], res(0, k).rearrange("p (r c) -> p r c", c=W)
                                 ).then_inc(out_sent[k], 16)
                    sp.wait_ge(fin_b, n + 1)
                    sp.dma_start(out[b, CA:C, rows, :], res(1, k).rearrange("p (r c) -> p r c", c=W)
                                 ).then_inc(out_sent[k], 16)

                chunk_loop(sp, b, send)
                for k in range(2):
                    sp.wait_ge(out_sent[k], b * (16 * NCH) + 16 * NCH)
                sp.sem_inc(image_sent, 1)

        @block.tensor
        def _(pe):
            mm = nc.tensor.matmul
            pe.wait_ge(const_in, 16 * len(loads))
            pe.wait_ge(sbuf_zero, 1)
            pe.wait_ge(psum_zero, 1)
            for k in range(N * N // 512):
                for t in range(2):
                    if k:
                        pe.wait_ge(hid_relu, 2 * k + t - 1)
                    mm(b_t[:, t * 512:(t + 1) * 512], mw1[:, t * 128:(t + 1) * 128],
                       rp[:, k * 512:(k + 1) * 512], start=True, stop=True).then_inc(hid_mm, 1)
            pe.wait_ge(hid_relu, 2 * (N * N // 512))
            for m in range(N):
                for t in range(2):
                    for side in range(2):
                        mm(b_q[side * N:(side + 1) * N, m * NH:(m + 1) * NH], hid[:, t, m * N:(m + 1) * N],
                           mw2[:, t, :], start=(m == 0 and t == 0), stop=False, skip_group_check=True)
            mm(b_q[:, 0:N * NH], ones[0:1, :], mb2, start=False, stop=True,
               skip_group_check=True).then_inc(pos_mm, 1)
            for t in range(NT):
                pe.wait_ge(gsel_done, t + 1)
                rhs = gsel[:, :, :].rearrange("p s i -> p (s i)")
                if t:
                    pe.wait_ge(spread_out, t)
                mm(b_v[:, 0:2 * NIMG], spread[:, 0:CA], rhs, start=True, stop=True)
                mm(b_v[:, 64:64 + 2 * NIMG], spread[:, CA:256], rhs, start=True, stop=True).then_inc(spread_mm, 1)

            with pe.Fori(0, B) as b:
                pe.wait_ge(norm0_w, b + 1)
                for o, lo in zip(half, (0, HALF)):
                    mm(o, ones[0:1, :], qkvb[:, lo:lo + HALF], start=True, stop=False)
                    mm(o, negmean[:, 0, :], wn[:, 0, lo:lo + HALF], start=False, stop=False)
                    last = mm(o, negmean[0:CB, 1, :], wn[0:CB, 1, lo:lo + HALF], start=False, stop=True)
                last.then_inc(bias_mm, 1)
                pe.wait_ge(bias_done, b + 1)

                def stages(j, g, s, on):
                    if on(3):
                        pe.wait_ge(norm_done, g - 2)
                        if on(4):
                            pe.wait_ge(yT_out, g - 3)
                        for t in range(3):
                            last = nc.tensor.transpose(
                                b_p[:, t * 128:(t + 1) * 128],
                                probs[:, (j - 3) % 2, 2 * t:2 * t + 2, :].rearrange("p h m -> p (h m)"), ident[:, :])
                        last.then_inc(pT_mm, 1)
                    if on(0):
                        pe.wait_ge(xl_done, g + 1)
                        pe.wait_ge(xhl_done, g + 1)
                        e = j % 2
                        products = [(xh[:, e, :], wnh, 0), (xl[:, e, :], wnh, 0), (xh[:, e, :], wnl, 0),
                                    (xhb[:, e, :], wnh, 1), (xhl[:, e, :], wnl, 1)]
                        for o, lo in zip(half, (0, HALF)):
                            if lo and on(1):
                                pe.wait_ge(vT_out, g)
                            for n, (xx, ww, t) in enumerate(products):
                                last = mm(o, xx, ww[:, t, lo:lo + HALF], start=(n == 0), stop=(n == 4))
                        last.then_inc(qkv_mm, 1)
                    if on(4):
                        pe.wait_ge(yT_out, g - 3)
                        if on(5):
                            pe.wait_ge(x1_done, g - 4)
                        ya = yT[:, 0:128].rearrange("p (w r c) -> p r w c", w=2, c=WS)
                        yb = yT[0:CB, 128:256].rearrange("p (w r c) -> p r w c", w=2, c=WS)
                        mm(b_r[:, 0:128], wp[:, 0, 0:CA], ya, start=True, stop=False)
                        mm(b_r[:, 0:128], wp[0:CB, 1, 0:CA], yb, start=False, stop=True)
                        mm(b_r[0:CB, 128:256], wp[:, 0, CA:C], ya, start=True, stop=False)
                        mm(b_r[0:CB, 128:256], wp[0:CB, 1, CA:C], yb, start=False, stop=True).then_inc(proj_mm, 1)
                    if on(1):
                        pe.wait_ge(prod_done, g * 2)
                        if on(2):
                            pe.wait_ge(oT_out, g - 1)
                        for t in range(3):
                            last = mm(b_o[:, t * N:(t + 1) * N],
                                      prod[:, t, :, :, :].rearrange("p h w d -> p (h w d)"), inv[:, :],
                                      start=True, stop=True)
                        last.then_inc(o_mm, 1)
                    if on(0):
                        for win in range(2):
                            pe.wait_ge(lo_out, g * 2 + win + 1)
                            if win and not on(1):
                                pe.wait_ge(v_out, g + 1)
                            o = b_t[0:NF, win * 512:win * 512 + 2 * C]
                            mm(o, fwdh[:, :], qk[:, win, :], start=True, stop=False)
                            mm(o, fwdl[:, :], qk[:, win, :], start=False, stop=True).then_inc(t_mm, 1)
                    if on(3):
                        pe.wait_ge(pT_out, g - 2)
                        pe.wait_ge(vbd_act, g - 2)
                        pe.wait_ge(vbd_dve, g - 2)
                        for t in range(3):
                            p, c = (t % 2) * 64, (t // 2) * 128
                            for win in range(2):
                                last = mm(b_p[p:p + 64, c + win * N:c + (win + 1) * N], vbd[:, (j - 3) % 4, win, t, :],
                                          probsT[:, t, win, :], start=True, stop=True)
                        last.then_inc(y_mm, 1)
                    if on(1):
                        pe.wait_ge(vT_out, g)
                        pe.wait_ge(oT_out, g)
                        if on(2):
                            pe.wait_ge(s_out, g - 1)
                        if on(0):
                            pe.wait_ge(v_out, g + 1)
                        for t in range(3):
                            last = mm(b_s[:, t * 128:(t + 1) * 128], obd[:, t, :, :].rearrange("p w n -> p (w n)"),
                                      vT[:, t, :, :].rearrange("p h m -> p (h m)"), start=True, stop=True)
                        last.then_inc(s_mm, 1)
                    if on(0):
                        for t in range(3):
                            last = nc.tensor.transpose(
                                b_v[:, HALF + t * N:HALF + (t + 1) * N],
                                vt[:, j % 2, t, :, :, :].rearrange("p h w d -> p (h w d)"), ident[0:N, 0:N])
                        last.then_inc(vT_mm, 1)

                pair_loop(pe, b, stages)

                def channels(weights, field, width):
                    rhs = sm[:, field:field + width, :]
                    mm(b_v[:, 0:width], weights[:, 0, 0:CA], rhs[:, :, 0], start=True, stop=False)
                    mm(b_v[:, 0:width], weights[0:CB, 1, 0:CA], rhs[0:CB, :, 1], start=False, stop=True)
                    mm(b_v[0:CB, 64:64 + width], weights[:, 0, CA:C], rhs[:, :, 0], start=True, stop=False)
                    return mm(b_v[0:CB, 64:64 + width], weights[0:CB, 1, CA:C], rhs[0:CB, :, 1], start=False, stop=True)

                pe.wait_ge(st_mean, b + 1)
                channels(mates, 0, 2).then_inc(mean_mm, 1)
                pe.wait_ge(st_dev, b + 1)
                channels(mates, 4, 1).then_inc(dev_mm, 1)
                pe.wait_ge(norm1_w, b + 1)
                channels(mn, 2, 1).then_inc(mbias_mm, 1)

                def merge(k, n, q, first):
                    pe.wait_ge(z_done, n + 1)
                    if not first:
                        pe.wait_ge(fin_a, n - 1)
                        pe.wait_ge(fin_b, n - 1)
                    for o, lo, hi in ((b_t[:, k * 512:k * 512 + CE], 0, CA), (b_s[0:CB, k * 512:k * 512 + CE], CA, C)):
                        mm(o, mn[:, 0, lo:hi], z(0, k), start=True, stop=False)
                        last = mm(o, mn[0:CB, 1, lo:hi], z(1, k), start=False, stop=True)
                    last.then_inc(merge_mm, 1)

                chunk_loop(pe, b, merge)

        @block.vector
        def _(dve):
            V = nc.vector
            V.memset(b_o[:, :], 0.0).then_inc(psum_zero, 1)
            chain = [0, 0]

            def link(ins):
                chain[1] += 1
                ins.then_inc(dve_chain, 1)
                dve.wait_ge(dve_chain, chain[0] + chain[1])

            def rstd(var, sd, r, t, wait):
                link(V.tensor_scalar(var, var, EPS, None, ALU.add))
                V.tensor_copy(t, var).then_inc(var_done, 1)
                dve.wait_ge(sqrt_done, wait)
                link(V.reciprocal(r, sd))
                link(V.tensor_tensor(t, var, r, ALU.mult))
                link(V.tensor_tensor(t, t, r, ALU.mult))
                link(V.tensor_scalar(t, t, -0.5, 1.5, ALU.mult, ALU.add))
                link(V.tensor_tensor(r, r, t, ALU.mult))

            dve.wait_ge(const_in, 16 * len(loads))
            dve.wait_ge(sbuf_zero, 1)
            link(V.tensor_copy(fwdh[:, :], fwd))
            V.tensor_tensor(fwdl[:, :], fwd, fwdh[:, :].bitcast(F32), ALU.subtract)
            V.tensor_scalar(wnh[CB:128, 1, :], ones[CB:128, 0:1].broadcast_to([CB, 3 * C]), 0.0, None, ALU.mult)
            for e in range(2):
                last = V.tensor_scalar(xhb[CB:128, e, :], ones[CB:128, :], 0.0, None, ALU.mult)
            link(last)
            for e in range(2):
                for row in BIAS_ROWS:
                    last = V.tensor_copy(xhb[row:row + 1, e, :], ones[row:row + 1, :])
            link(last)
            for t in range(NT):
                for c in range(NL):
                    n = t * NL + c
                    dve.wait_ge(ld_in[n % NLOAD], 16 * (n // NLOAD + 1))
                    for i in range(LOAD // STAT):
                        last = V.bn_stats(bn0[:, c * (LOAD // STAT) + i, :], ld[:, n % NLOAD, i * STAT:(i + 1) * STAT])
                    last.then_inc(ld_read, 1)
                dve.wait_ge(ld_read, (t + 1) * NL)
                link(V.bn_aggr(gst[:, 0:2], bn0[:, :, :].rearrange("p k n -> p (k n)")))
                rstd(gst[:, 1:2], gst[:, 2:3], gst[:, 3:4], gst[:, 4:5], t + 1)
                V.tensor_scalar(gsel[:, 0, :], image[:, :], gst[:, 0:1], None, ALU.mult)
                V.tensor_scalar(gsel[:, 1, :], image[:, :], gst[:, 3:4], None, ALU.mult).then_inc(gsel_done, 1)
                dve.wait_ge(spread_mm, t + 1)
                to = st0[:, :, :, t * NIMG:(t + 1) * NIMG]
                V.tensor_copy(to[:, 0], b_v[:, 0:2 * NIMG].rearrange("p (s i) -> p s i", s=2))
                link(V.tensor_copy(to[:, 1], b_v[:, 64:64 + 2 * NIMG].rearrange("p (s i) -> p s i", s=2)))
                if t + 1 < NT:
                    V.tensor_copy(gst[:, 7:8], gst[:, 0:1]).then_inc(spread_out, 1)
            dve.wait_ge(pos_mm, 1)
            link(V.tensor_copy(posb[:, :, :], b_q[:, 0:N * NH].rearrange("p (m h) -> p h m", h=NH)))
            chained = chain[1]

            with dve.Fori(0, B) as b:
                PER_IMAGE = 17
                chain[0], chain[1] = b * PER_IMAGE, chained
                for t in range(2):
                    last = V.tensor_scalar(wn[:, t, :], wq[:, t, :], st0[:, t, 1, bass.ds(b, 1)], None, ALU.mult)
                link(last)
                V.tensor_copy(wnh[:, 0, :], wn[:, 0, :])
                V.tensor_copy(wnh[0:CB, 1, :], wn[0:CB, 1, :])
                link(V.tensor_copy(wnl[CB:128, 1, :], wn[CB:128, 1, :]))
                V.tensor_tensor(wnl[:, 0, :], wn[:, 0, :], wnh[:, 0, :].bitcast(F32), ALU.subtract)
                V.tensor_tensor(wnl[0:CB, 1, :], wn[0:CB, 1, :], wnh[0:CB, 1, :].bitcast(F32), ALU.subtract)
                for t in range(2):
                    last = V.tensor_scalar(negmean[:, t, :], ones[:, :], st0[:, t, 0, bass.ds(b, 1)], -1.0,
                                           ALU.mult, ALU.mult)
                last.then_inc(norm0_w, 1)
                dve.wait_ge(bias_mm, b + 1)
                first, second = (slice(row, row + 1) for row in BIAS_ROWS)
                halves = "p (k c) -> p k c"
                V.tensor_copy(wnh[first, 1, :].rearrange(halves, k=2), b_q[first].rearrange(halves, k=2)[:, :, 0:HALF])
                link(V.tensor_copy(biasrow[second].bitcast(F32R).rearrange(halves, k=2),
                                   b_q[second].rearrange(halves, k=2)[:, :, 0:HALF]))
                link(V.tensor_tensor(wnh[second, 1, :].rearrange(halves, k=2),
                                     b_q[second].rearrange(halves, k=2)[:, :, 0:HALF],
                                     biasrow[second].rearrange(halves, k=2), ALU.subtract))
                V.tensor_copy(biasrow[0:1, 0:1], ones[0:1, 0:1]).then_inc(bias_done, 1)

                def tokens(win):
                    return slice(win * N, (win + 1) * N)

                def stages(j, g, s, on):
                    if on(0):
                        vv = vt[:, j % 2, :, :, :, :]

                        def values(win):
                            return V.tensor_copy(
                                vv[:, :, :, win, :].rearrange("p t h d -> p (t h) d")
                                .rearrange("p (k x) d -> p k x d", k=2),
                                b_q[tokens(win)].rearrange("p (k c) -> p k c", k=2)[:, :, C:HALF]
                                .rearrange("p k (x d) -> p k x d", d=HD))

                        def rest(win):
                            dve.wait_ge(hi_out, g * 2 + win + 1)
                            V.tensor_tensor(qk[tokens(1 - win), win, :].rearrange("p (k c) -> p k c", k=2),
                                            b_q[tokens(win)].rearrange("p (k c) -> p k c", k=2)[:, :, 0:C],
                                            qk[tokens(win), win, :].bitcast(F32).rearrange("p (k c) -> p k c", k=2),
                                            ALU.subtract).then_inc(lo_out, 1)

                        dve.wait_ge(qkv_mm, g + 1)
                        values(1).then_inc(v1_out, 1)
                        rest(0)
                        rest(1)
                    if on(2):
                        dve.wait_ge(exp_done, g - 1)
                        V.tensor_reduce(ssum[:, j % 2, :], probs[:, j % 2, :, :], AX.X, ALU.add
                                        ).then_inc(sum_done, 1)
                    if on(0):
                        values(0).then_inc(v_out, 1)
                    if on(2):
                        dve.wait_ge(sum_done, g - 1)
                        V.reciprocal(srec[:, j % 2, :], ssum[:, j % 2, :]).then_inc(rec_done, 1)

                    if on(4):
                        i = j - 4
                        row, col, k = (s + i // SPAIRS) * WS + 1, (i % SPAIRS) * 16, (i % UN) // SPAIRS
                        dve.wait_ge(proj_mm, g - 3)
                        for t, n, xt in ((0, CA, x1a), (1, CB, x1b)):
                            last = V.scalar_tensor_tensor(
                                out=xt[:, bass.ds(row, WS), col + 1:col + 17],
                                in0=b_r[0:n, t * 128:(t + 1) * 128].rearrange("p (r c) -> p r c", c=16),
                                scalar=pb[0:n, t:t + 1],
                                in1=xs[0:n, t, k, :].rearrange("p (r c) -> p r c", c=W)[:, :, col:col + 16],
                                op0=ALU.add, op1=ALU.add)
                        last.then_inc(x1_done, 1)

                def late(j, g, s, on):
                    if on(1):
                        pr = probs[:, (j - 1) % 2, :, :]
                        dve.wait_ge(s_mm, g)
                        V.tensor_tensor(pr, b_s[:, 0:NH * N].rearrange("p (h m) -> p h m", m=N), posb[:, :, :],
                                        ALU.add).then_inc(s_out, 1)
                    if on(1):
                        dve.wait_ge(s_out, g)
                        V.tensor_reduce(smax[:, (j - 1) % 2, :], pr, AX.X, ALU.max).then_inc(max_done, 1)
                    if on(0):
                        for win in range(2):
                            dve.wait_ge(qh_out, g * 2 + win + 1)
                            V.tensor_tensor(prod[:, :, :, win, :].rearrange("p t h d -> p (t h) d"),
                                            qh[:, win, :].rearrange("p (h d) -> p h d", d=HD),
                                            b_t[0:NF, win * 512 + C:win * 512 + 2 * C]
                                            .rearrange("p (h d) -> p h d", d=HD), ALU.mult).then_inc(prod_done, 1)
                    if on(0):
                        dve.wait_ge(v_out, g + 1)
                        V.tensor_copy(vbd[0:N, j % 4, :, :, 0:HD],
                                      vt[:, j % 2, :, 0, :, :].rearrange("p t w d -> p w t d")).then_inc(vbd_dve, 1)
                    for part in range(4):
                        final = not on(0) and j == 3
                        i = j - 4 if final else j - 4 - part
                        if i % SPAIRS == SPAIRS - 1 and on(j - i) and (final or on(0)):
                            if part == 0:
                                dve.wait_ge(x1_done, g - 3)
                            t, q = part // 2, part % 2
                            n, xt = ((CA, x1a), (CB, x1b))[t]
                            strip = s + i // SPAIRS
                            V.bn_stats(bn1[0:n, t, bass.ds(strip * 2 + q, 1), :],
                                       xt[:, bass.ds(strip * WS + q * ROWS + 1, ROWS), 1:W + 1])

                def second_part(j, g, s, on):
                    k, c = j // SPAIRS, (j % SPAIRS) * 2
                    dve.wait_ge(xh_done, g + 1)
                    V.tensor_tensor(xhl[CB:128, j % 2, :].rearrange("p (w r c) -> p w r c", w=2, c=WS),
                                    pixels(1, k, c),
                                    xhl[0:CB, j % 2, :].bitcast(F32).rearrange("p (w r c) -> p w r c", w=2, c=WS),
                                    ALU.subtract).then_inc(xhl_done, 1)

                pair_loop(dve, b, ahead(stages, second_part, late), LAST + 1)

                link(V.memset(sm[:, 7, :], 0.0))
                V.memset(sm[:, 6, :], 0.0)
                for t, n in ((0, CA), (1, CB)):
                    last = V.bn_aggr(sm[0:n, 0:2, t], bn1[0:n, t, :, :].rearrange("p k n -> p (k n)"))
                last.then_inc(st_mean, 1)
                dve.wait_ge(mean_mm, b + 1)
                V.tensor_copy(sm[:, 2:4, 0], b_v[:, 0:2])
                link(V.tensor_copy(sm[0:CB, 2:4, 1], b_v[0:CB, 64:66]))
                link(V.tensor_tensor(sm[:, 4, :], sm[:, 0, :], sm[:, 2, :], ALU.subtract))
                V.tensor_tensor(sm[:, 4, :], sm[:, 4, :], sm[:, 4, :], ALU.mult).then_inc(st_dev, 1)
                dve.wait_ge(dev_mm, b + 1)
                link(V.tensor_tensor(sm[:, 5, 0:1], b_v[:, 0:1], sm[:, 3, 0:1], ALU.add))
                link(V.tensor_tensor(sm[0:CB, 5, 1:2], b_v[0:CB, 64:65], sm[0:CB, 3, 1:2], ALU.add))
                rstd(sm[:, 5, :], sm[:, 6, :], sm[:, 7, :], sm[:, 4, :], b + NT + 1)
                for t, n, xt in ((0, CA, x1a), (1, CB, x1b)):
                    last = V.tensor_scalar(mn[0:n, t, :], wm[0:n, t, :], sm[0:n, 7, t:t + 1], None, ALU.mult)
                    for edge in (0, PW - 1):
                        V.tensor_scalar(xt[:, :, edge], ones[0:n, 0:1].broadcast_to([n, H + 2]), sm[0:n, 2, t:t + 1],
                                        None, ALU.mult)
                    for edge in (0, H + 1):
                        last = V.tensor_scalar(xt[:, edge, 1:PW - 1], ones[0:n, 0:1].broadcast_to([n, W]),
                                               sm[0:n, 2, t:t + 1], None, ALU.mult)
                last.then_inc(norm1_w, 1)
                dve.wait_ge(mbias_mm, b + 1)
                link(V.tensor_tensor(mc[:, 0:1], mb[:, 0:1], b_v[:, 0:1], ALU.subtract))
                link(V.tensor_tensor(mc[0:CB, 1:2], mb[0:CB, 1:2], b_v[0:CB, 64:65], ALU.subtract))
                V.tensor_copy(sm[:, 4, :], mc[:, :]).then_inc(mc_done, 1)

                assert chain[1] - chained == PER_IMAGE

                def stencil(k, n, q, first):
                    rows = bass.ds(q * ROWS + 1, ROWS)
                    zz = [z(t, k).rearrange("p (r c) -> p r c", c=W) for t in range(2)]
                    dve.wait_ge(diag_done, n + 1)
                    for t, m in ((0, CA), (1, CB)):
                        dg = diag[0:m, t, k, :, :]
                        last = V.tensor_tensor(zz[t], dg[:, 0:ROWS, 0:W], dg[:, 1:, 1:], ALU.add)
                    last.then_inc(nb_done, 1)
                    dve.wait_ge(nb_done, n + 1)
                    for t, xt in ((0, x1a), (1, x1b)):
                        last = V.scalar_tensor_tensor(out=zz[t], in0=xt[:, rows, 1:W + 1], scalar=5.0, in1=zz[t],
                                                      op0=ALU.mult, op1=ALU.subtract)
                    last.then_inc(z_done, 1)

                def result(k, n, q, first):
                    dve.wait_ge(merge_mm, n + 1)
                    if not first:
                        dve.wait_ge(out_sent[k], n * 16 - k * 16)
                    for t, m, xt, o in ((0, CA, x1a, b_t), (1, CB, x1b, b_s)):
                        V.scalar_tensor_tensor(
                            out=res(t, k).rearrange("p (r c) -> p r c", c=W),
                            in0=o[0:m, k * 512:k * 512 + CE].rearrange("p (r c) -> p r c", c=W),
                            scalar=mc[0:m, t:t + 1], in1=xt[:, bass.ds(q * ROWS + 1, ROWS), 1:W + 1],
                            op0=ALU.add, op1=ALU.add).then_inc(fin_a if t == 0 else fin_b, 1)

                n0 = b * NCH
                stencil(0, n0, 0, True)
                stencil(1, n0 + 1, 1, True)
                result(0, n0, 0, True)
                with dve.Fori(1, NCH // 2) as d:
                    n, q = b * NCH + d * 2, d * 2
                    stencil(0, n, q, False)
                    result(1, n - 1, q - 1, None)
                    stencil(1, n + 1, q + 1, False)
                    result(0, n, q, False)
                result(1, n0 + NCH - 1, NCH - 1, False)

        @block.scalar
        def _(act):
            A = nc.scalar

            def copy(o, i):
                return A.activation(o, i, ACT.Copy)

            for k in range(N * N // 512):
                for t in range(2):
                    act.wait_ge(hid_mm, 2 * k + t + 1)
                    A.activation(hid[:, t, k * 512:(k + 1) * 512], b_t[:, t * 512:(t + 1) * 512], ACT.Relu,
                                 bias=mb1[:, t:t + 1]).then_inc(hid_relu, 1)
            for t in range(NT):
                act.wait_ge(var_done, t + 1)
                A.activation(gst[:, 2:3], gst[:, 1:2], ACT.Sqrt).then_inc(sqrt_done, 1)

            act.wait_ge(sbuf_zero, 1)
            with act.Fori(0, B) as b:
                def first_part(j, g, s, on):
                    k, c = j // SPAIRS, (j % SPAIRS) * 2
                    if j % SPAIRS == 0:
                        act.wait_ge(strip_in[k], b * (NB * 32) + s * 16 + 32)
                    if on(2):
                        act.wait_ge(qkv_mm, g - 1)
                    for t, o in ((0, xh), (1, xhb), (1, xhl)):
                        last = copy(o[0:CA if t == 0 else CB, j % 2, :].rearrange("p (w r c) -> p w r c", w=2, c=WS),
                                    pixels(t, k, c))
                    last.then_inc(xh_done, 1)

                def stages(j, g, s, on):
                    if on(3):
                        act.wait_ge(pT_mm, g - 2)
                        copy(probsT[:, :, :, :].rearrange("p t w n -> p (t w n)"), b_p[:, 0:NH * N]).then_inc(pT_out, 1)
                    if on(0):
                        act.wait_ge(qkv_mm, g + 1)
                        for win in range(2):
                            if win:
                                act.wait_ge(v1_out, g + 1)
                            rows = slice(win * N, (win + 1) * N)
                            copy(qk[rows, win, :].rearrange("p (k c) -> p k c", k=2),
                                 b_q[rows].rearrange("p (k c) -> p k c", k=2)[:, :, 0:C]).then_inc(hi_out, 1)
                    if on(2):
                        act.wait_ge(sub_done, g - 1)
                        pr = probs[:, j % 2, :, :].rearrange("p h m -> p (h m)")
                        A.activation(pr, pr, ACT.Exp).then_inc(exp_done, 1)
                    if on(1):
                        act.wait_ge(o_mm, g)
                        for p in range(0, 128, HD):
                            last = copy(obd[p:p + HD, :, p // HD % 2, :],
                                        b_o[p:p + HD, 0:3 * N].rearrange("p (t n) -> p t n", n=N))
                        last.then_inc(oT_out, 1)

                def late(j, g, s, on):
                    if on(3):
                        act.wait_ge(y_mm, g - 2)
                        copy(yT[:, :], b_p[:, 0:256]).then_inc(yT_out, 1)
                    if on(0):
                        for win in range(2):
                            act.wait_ge(t_mm, g * 2 + win + 1)
                            copy(qh[:, win, :], b_t[0:NF, win * 512:win * 512 + C]).then_inc(qh_out, 1)
                    if on(0):
                        act.wait_ge(v_out, g + 1)
                        copy(vbd[N:128, j % 4, :, :, HD:], vt[:, j % 2, :, 1, :, :].rearrange("p t w d -> p w t d")
                             ).then_inc(vbd_act, 1)
                        act.wait_ge(vT_mm, g + 1)
                        for h in range(2):
                            rows = slice(h * 64, h * 64 + 64)
                            last = copy(vT[rows, :, h, :],
                                        b_v[rows, HALF:HALF + 3 * N].rearrange("p (t m) -> p t m", m=N))
                        last.then_inc(vT_out, 1)

                pair_loop(act, b, ahead(stages, first_part, late), LAST + 1)
                act.wait_ge(var_done, b + NT + 1)
                A.activation(sm[:, 6, :], sm[:, 5, :], ACT.Sqrt).then_inc(sqrt_done, 1)

        @block.gpsimd
        def _(pool):
            P = nc.gpsimd
            pool.wait_ge(const_in, 16 * len(loads))
            P.memset(ones[:, :], 1.0)
            P.memset(obd[:, :, :, :], 0.0)
            P.memset(vT[:, :, :, :], 0.0)
            P.memset(mc[:, :], 0.0)
            P.memset(sm[:, :, :], 0.0)
            P.memset(vbd[:, :, :, :, :], 0.0).then_inc(sbuf_zero, 1)
            with pool.Fori(0, B) as b:
                def stages(j, g, s, on):
                    if on(2):
                        pr = probs[:, j % 2, :, :]
                        pool.wait_ge(max_done, g - 1)
                        P.tensor_tensor(pr, pr, smax[:, j % 2, :].unsqueeze(2).broadcast_to([128, NH, N]),
                                        ALU.subtract).then_inc(sub_done, 1)
                        pool.wait_ge(rec_done, g - 1)
                        P.tensor_tensor(pr, pr, srec[:, j % 2, :].unsqueeze(2).broadcast_to([128, NH, N]),
                                        ALU.mult).then_inc(norm_done, 1)

                def second_part(j, g, s, on):
                    k, c = j // SPAIRS, (j % SPAIRS) * 2
                    pool.wait_ge(xh_done, g + 1)
                    P.tensor_tensor(xl[:, j % 2, :].rearrange("p (w r c) -> p w r c", w=2, c=WS), pixels(0, k, c),
                                    xh[:, j % 2, :].bitcast(F32).rearrange("p (w r c) -> p w r c", w=2, c=WS),
                                    ALU.subtract).then_inc(xl_done, 1)

                pair_loop(pool, b, ahead(stages, second_part, lambda *a: None), LAST + 1)
                pool.wait_ge(norm1_w, b + 1)

                def diagonals(k, n, q, first):
                    if not first:
                        pool.wait_ge(nb_done, n - 1)
                    for t, m, xt in ((0, CA, x1a), (1, CB, x1b)):
                        last = P.tensor_tensor(diag[0:m, t, k, :, :], xt[:, bass.ds(q * ROWS + 1, ROWS + 1), 0:W + 1],
                                               xt[:, bass.ds(q * ROWS, ROWS + 1), 1:W + 2], ALU.add)
                    last.then_inc(diag_done, 1)

                chunk_loop(pool, b, diagonals)


def halves(qk, v):
    return np.concatenate([qk[:C], v[:C // 2], qk[C:], v[C // 2:]])


def kernel(**inputs):
    import concourse.bacc as bacc
    from concourse.bass_utils import run_bass_kernel_spmd

    a = {k: np.asarray(v) for k, v in inputs.items()}
    x = a["x"]
    arrays = {
        "x": x,
        "wqkvT": np.ascontiguousarray(halves(a["L0_conv_QK_w"], a["L0_conv_V_w"]).T),
        "qkvb": halves(a["L0_conv_QK_b"], a["L0_conv_V_b"])[None],
        "projT": np.ascontiguousarray(a["L0_conv_proj_w"].T),
        "projb": a["L0_conv_proj_b"][:, None],
        "mergeT": np.ascontiguousarray(a["L1_conv_merge_w"][:, :, 0, 0].T),
        "mergeb": a["L1_conv_merge_b"][:, None],
        "w1": a["L0_conv_meta_w1"],
        "b1": np.ascontiguousarray(a["L0_conv_meta_b1"].reshape(-1, 128).T),
        "w2": a["L0_conv_meta_w2"],
        "b2": np.tile(a["L0_conv_meta_b2"], N)[None],
    }
    for name, value in constants(x.shape[0]).items():
        arrays[name] = np.ascontiguousarray(value, dtype=np.float32)
    nc = bacc.Bacc("TRN2", target_bir_lowering=False, num_devices=1)
    w = {name: nc.dram_tensor("in_" + name, value.shape, F32, kind="ExternalInput").ap()
         for name, value in arrays.items()}
    out = nc.dram_tensor("out", x.shape, F32, kind="ExternalOutput").ap()
    program(nc, w["x"], out, w)
    r = run_bass_kernel_spmd(nc, [{"in_" + name: value for name, value in arrays.items()}], core_ids=[0])
    return r.results[0]["out"]
```

```python
from contextlib import ExitStack

import numpy as np

import concourse.bass as bass
from concourse import mybir

F32 = mybir.dt.float32
F32R = mybir.dt.float32r
ALU = mybir.AluOpType
ACT = mybir.ActivationFunctionType
AX = mybir.AxisListType

C = 192
CA, CB = 128, 64
NH, HD, WS = 6, 32, 8
N = WS * WS
G, CG = 32, 6
EPS = 1e-5
NF = 94
HID = 256
ROWS = 4
STAT = 512
LOAD = 4096
HALF = 3 * C // 2
BIAS_ROWS = (64, 96)
NLOAD = 3


def fourier():
    n = np.arange(WS)
    rows, cols = np.meshgrid(n, n, indexing="ij")
    forward, inverse = [], []
    scale = HD ** -0.5 / N
    for u in range(WS):
        for v in range(WS):
            if (-u % WS, -v % WS) < (u, v):
                continue
            theta = (2 * np.pi / WS * ((u * rows + v * cols) % WS)).ravel()
            c, s = np.cos(theta), np.sin(theta)
            if (-u % WS, -v % WS) == (u, v):
                forward.append(np.round(c))
                inverse.append(scale * np.round(c))
            else:
                forward += [c, -s, c - s]
                inverse += [2 * scale * (c + s), 2 * scale * (s - c), -2 * scale * s]
    return np.array(forward).T, np.array(inverse)


def constants(B):
    forward, inverse = fourier()
    coords = np.stack(np.meshgrid(np.arange(WS), np.arange(WS), indexing="ij")).reshape(2, -1)
    rp = (coords[:, :, None] - coords[:, None, :]).astype(np.float32)
    rp = np.sign(rp) * np.log1p(np.abs(rp))
    channel, group = np.arange(C), np.arange(min(B * G, 128))
    return {
        "fwd": np.tile(forward, (2, 1)),
        "inv": inverse,
        "rp": rp.transpose(0, 2, 1).reshape(2, N * N),
        "ident": np.eye(128),
        "spread": group[:, None] % G == np.concatenate([channel, channel[CA:]])[None] // CG,
        "image": group[:, None] // G == np.arange(len(group) // G)[None],
        "mates": (channel[:, None] // CG == channel[None] // CG) / CG,
    }


def program(nc, x, out, w):
    B, _, H, W = x.shape
    assert W == 128 and H % 16 == 0 and H // ROWS % 4 == 0
    NP = H * W // 128
    SPAIRS = W // 16
    UN = 2 * SPAIRS
    NB = NP // UN
    LAST = 4
    PW = W + 2
    NCH = H // ROWS
    CE = ROWS * W
    TG = min(B * G, 128)
    NT = B * G // TG
    NIMG = TG // G
    GS = CG * H * W
    NL = GS // LOAD
    assert NL % NLOAD == 0

    with ExitStack() as ctx:
        def sb(name, shape, dtype=F32):
            return ctx.enter_context(nc.sbuf_tensor(name, shape, dtype))

        def ps(name, banks):
            return ctx.enter_context(nc.psum_tensor(name, [128, 512 * banks], F32))

        def sem(name):
            return ctx.enter_context(nc.semaphore(name))

        plane = (H + 2) * PW
        x1 = sb("x1", [128, max(2 * plane, 3 * N * N + NLOAD * LOAD + GS // STAT * 6 + 768)])
        x1a = x1[:, 0:plane].rearrange("p (r c) -> p r c", c=PW)
        x1b = x1[0:CB, plane:2 * plane].rearrange("p (r c) -> p r c", c=PW)
        xs = sb("xs", [128, 2, 2, WS * W])
        wq = sb("wq", [128, 2, 3 * C])
        wnh, wnl = sb("wnh", [128, 2, 3 * C], F32R), sb("wnl", [128, 2, 3 * C], F32R)
        wp = sb("wp", [128, 2, C])
        wm = sb("wm", [128, 2, C])
        mn = sb("mn", [128, 2, C])
        qkvb = sb("qkvb_row", [1, 3 * C])
        shared = sb("shared", [128, 2688])
        at = [0]

        def share(*dims):
            n = int(np.prod(dims))
            at[0] += n
            a = shared[:, at[0] - n:at[0]]
            if len(dims) == 1:
                return a
            names = "abcd"[:len(dims)]
            return a.rearrange(f"p ({' '.join(names)}) -> p {' '.join(names)}", **dict(zip(names, dims)))

        probs = share(2, NH, N)
        probsT = share(3, 2, N)
        qh, prod = share(2, C)[0:NF], share(3, 2, 2, HD)[0:NF]
        bn1 = share(2, 2 * NCH, 6)
        wn = shared[:, 0:6 * C].rearrange("p (t n) -> p t n", t=2)
        negmean = shared[:, 6 * C:6 * C + 256].rearrange("p (t n) -> p t n", t=2)
        biasrow = shared[:, 6 * C + 256:9 * C + 256]
        assert max(at[0], 9 * C + 256) <= 2688
        diag = shared[:, 0:4 * (ROWS + 1) * (W + 1)].rearrange("p (t k r c) -> p t k r c", t=2, k=2, c=W + 1)
        pb, mb, mc = sb("pb", [128, 2]), sb("mb", [128, 2]), sb("mc", [128, 2])
        fwdh, fwdl = sb("fwdh", [128, NF], F32R), sb("fwdl", [128, NF], F32R)
        inv = sb("inv_sb", [NF, N])
        ident, ones = sb("ident_sb", [128, 128]), sb("ones", [128, 128])
        spread, image = sb("spread_sb", [TG, 256]), sb("image_sb", [TG, NIMG])
        mates = sb("mates_sb", [128, 2, C])
        posb = sb("posb", [128, NH, N])
        gst, gsel = sb("gst", [TG, 8]), sb("gsel", [TG, 2, NIMG])
        st0 = sb("st0", [128, 2, 2, B + 1])
        sm = sb("sm", [128, 8, 2])
        xh, xl, xhl = (sb(name, [128, 2, 128], F32R) for name in ("xh", "xl", "xhl"))
        xhb = sb("xhb", [128, 2, 128], F32R)
        vt = sb("vt", [N, 2, 3, 2, 2, HD])
        vbd = sb("vbd", [128, 4, 2, 3, 64])
        vT = sb("vT", [128, 3, 2, N])
        obd = sb("obd", [128, 3, 2, N])
        yT = sb("yT", [128, 256])
        qk = sb("qk", [128, 2, 2 * C], F32R)
        smax, ssum, srec = sb("smax", [128, 2, NH]), sb("ssum", [128, 2, NH]), sb("srec", [128, 2, NH])

        rp = x1[0:2, 0:N * N]
        tail = 3 * N * N + NLOAD * LOAD + GS // STAT * 6
        fwd, mb1 = x1[:, tail:tail + NF], x1[:, tail + NF:tail + NF + 2]
        mw2 = x1[:, tail + NF + 2:][:, 0:2 * NH].rearrange("p (t h) -> p t h", t=2)
        mw1, mb2 = x1[0:2, tail + 128:tail + 128 + HID], x1[0:1, tail + 128 + HID:tail + 128 + HID + N * NH]
        hid = x1[:, N * N:3 * N * N].rearrange("p (t n) -> p t n", t=2)
        ld = x1[0:TG, 3 * N * N:3 * N * N + NLOAD * LOAD].rearrange("p (k n) -> p k n", k=NLOAD)
        bn0 = x1[0:TG, 3 * N * N + NLOAD * LOAD:][:, 0:GS // STAT * 6].rearrange("p (k n) -> p k n", n=6)

        def z(t, k):
            return xs[0:CA if t == 0 else CB, t, 0, k * CE:(k + 1) * CE]

        def x1_under(k):
            return xs[CB:128, 1, 0, k * CE:(k + 1) * CE]

        def res(t, k):
            return xs[0:CA if t == 0 else CB, t, 1, k * CE:(k + 1) * CE]

        b_q, b_t, b_o, b_s, b_p = ps("b_q", 2), ps("b_t", 2), ps("b_o", 1), ps("b_s", 2), ps("b_p", 1)
        half = [b_q[:, 0:HALF], b_q[:, 512:512 + HALF]]
        b_v = b_q[:, 512:1024]
        b_r = b_s[:, 512:1024]

        const_in = sem("const_in")
        z_free = sem("z_free")
        ld_in = [sem(f"ld_in{k}") for k in range(NLOAD)]
        strip_in = [sem(f"strip_in{k}") for k in range(2)]
        out_sent = [sem(f"out_sent{k}") for k in range(2)]
        sbuf_zero, hid_mm, hid_relu, pos_mm = map(sem, ("sbuf_zero", "hid_mm", "hid_relu", "pos_mm"))
        ld_read, gsel_done, spread_mm, spread_out = map(sem, ("ld_read", "gsel_done", "spread_mm", "spread_out"))
        dve_chain, var_done, sqrt_done = map(sem, ("dve_chain", "var_done", "sqrt_done"))
        norm0_w, bias_mm, bias_done = map(sem, ("norm0_w", "bias_mm", "bias_done"))
        border_w, mc_done, st_mean, st_dev, norm1_w, mean_mm, dev_mm, mbias_mm = map(sem, (
            "border_w", "mc_done", "st_mean", "st_dev", "norm1_w", "mean_mm", "dev_mm", "mbias_mm"))
        qkv_mm, t_mm, vT_mm, s_mm, pT_mm, y_mm, proj_mm, o_mm = map(sem, (
            "qkv_mm", "t_mm", "vT_mm", "s_mm", "pT_mm", "y_mm", "proj_mm", "o_mm"))
        v1_out, v_out, lo_out, prod_done, s_out, max_done, sum_done, rec_done, x1_done = map(sem, (
            "v1_out", "v_out", "lo_out", "prod_done", "s_out", "max_done", "sum_done", "rec_done", "x1_done"))
        (hi_out, xh_done, xl_done, xhl_done, qh_out, vT_out, exp_done, pT_out, yT_out, oT_out, vbd_act,
         vbd_dve) = map(sem, (
            "hi_out", "xh_done", "xl_done", "xhl_done", "qh_out", "vT_out", "exp_done", "pT_out", "yT_out", "oT_out",
            "vbd_act", "vbd_dve"))
        sub_done, norm_done = map(sem, ("sub_done", "norm_done"))
        diag_done, nb_done, z_done, under_done, merge_mm, fin_a, fin_b = map(sem, (
            "diag_done", "nb_done", "z_done", "under_done", "merge_mm", "fin_a", "fin_b"))

        loads = [
            (wq[:, 0], w["wqkvT"][0:CA]), (wq[0:CB, 1], w["wqkvT"][CA:C]),
            (wq[CB:128, 1], w["wqkvT"][CA:C]),
            (wp[:, 0], w["projT"][0:CA]), (wp[0:CB, 1], w["projT"][CA:C]),
            (wm[:, 0], w["mergeT"][0:CA]), (wm[0:CB, 1], w["mergeT"][CA:C]),
            (mates[:, 0], w["mates"][0:CA]), (mates[0:CB, 1], w["mates"][CA:C]),
            (pb[:, 0:1], w["projb"][0:CA]), (pb[0:CB, 1:2], w["projb"][CA:C]),
            (mb[:, 0:1], w["mergeb"][0:CA]), (mb[0:CB, 1:2], w["mergeb"][CA:C]),
            (qkvb[:, :], w["qkvb"]), (fwd, w["fwd"]),
            (inv[:, :], w["inv"]), (ident[:, :], w["ident"]), (spread[:, :], w["spread"]),
            (image[:, :], w["image"]), (rp, w["rp"]), (mw1, w["w1"]), (mb1, w["b1"]),
            (mw2, w["w2"].rearrange("(t p) h -> p t h", p=128)), (mb2, w["b2"]),
        ]

        def pair_loop(eng, b, stages, last=LAST):
            for j in range(UN):
                stages(j, b * NP + j, 0, lambda lag, j=j: lag <= j)
            with eng.Fori(1, NB) as d:
                for j in range(UN):
                    stages(j, b * NP + d * UN + j, d * 2, lambda lag: True)
            for j in range(last):
                stages(j, b * NP + NP + j, 2 * NB, lambda lag, j=j: lag > j)

        def ahead(early, first, late):
            def all_three(j, g, s, on):
                early(j - 1, g - 1, s, lambda lag: on(lag + 1))
                if on(0):
                    first(j, g, s, on)
                late(j - 1, g - 1, s, lambda lag: on(lag + 1))
            return all_three

        def chunk_loop(eng, b, stages):
            for q in range(4):
                stages(q % 2, b * NCH + q, q, q < 2)
            with eng.Fori(1, NCH // 4) as d:
                for q in range(4):
                    stages(q % 2, b * NCH + d * 4 + q, d * 4 + q, False)

        def pixels(t, k, c):
            return xs[0:CA if t == 0 else CB, t, k, :].rearrange("p (r w c) -> p w r c", r=WS, c=WS)[:, c:c + 2]

        block = ctx.enter_context(nc.Block())

        @block.sync
        def _(sp):
            for dst, src in loads:
                sp.dma_start(dst, src).then_inc(const_in, 16)
            xg = x.rearrange("b (g c) h w -> (b g) (c h w)", g=G)
            for t in range(NT):
                for c in range(NL):
                    n = t * NL + c
                    if n >= NLOAD:
                        sp.wait_ge(ld_read, n - NLOAD + 1)
                    sp.dma_start(ld[:, n % NLOAD, :], xg[t * TG:(t + 1) * TG, c * LOAD:(c + 1) * LOAD]
                                 ).then_inc(ld_in[n % NLOAD], 16)

            for k in range(2):
                sp.sem_inc(out_sent[k], 1)

            def strip(b, s, k):
                rows = bass.ds(s * WS, WS)
                sp.dma_start(xs[:, 0, k, :].rearrange("p (r c) -> p r c", c=W), x[b, 0:CA, rows, :]
                             ).then_inc(strip_in[k], 16)
                sp.dma_start(xs[0:CB, 1, k, :].rearrange("p (r c) -> p r c", c=W), x[b, CA:C, rows, :]
                             ).then_inc(strip_in[k], 16)

            with sp.Fori(0, B) as b:
                sp.wait_ge(z_free, b + 1)
                strip(b, 0, 0)
                for k in range(2):
                    sp.wait_ge(out_sent[k], b * (16 * NCH) + 1)
                strip(b, 1, 1)
                with sp.Fori(1, NB) as d:
                    for k in range(2):
                        sp.wait_ge(x1_done, b * NP + d * UN + ((k + 1) * SPAIRS - UN))
                        strip(b, d * 2 + k, k)

                def send(k, n, q, first):
                    rows = bass.ds(q * ROWS, ROWS)
                    sp.wait_ge(fin_a, n + 1)
                    sp.dma_start(out[b, 0:CA, rows, :], res(0, k).rearrange("p (r c) -> p r c", c=W)
                                 ).then_inc(out_sent[k], 16)
                    sp.wait_ge(fin_b, n + 1)
                    sp.dma_start(out[b, CA:C, rows, :], res(1, k).rearrange("p (r c) -> p r c", c=W)
                                 ).then_inc(out_sent[k], 16)

                chunk_loop(sp, b, send)

            for k in range(2):
                sp.wait_ge(out_sent[k], B * 16 * NCH + 1)

        @block.tensor
        def _(pe):
            mm = nc.tensor.matmul
            pe.wait_ge(const_in, 16 * len(loads))
            pe.wait_ge(sbuf_zero, 1)
            for k in range(N * N // 512):
                for t in range(2):
                    if k:
                        pe.wait_ge(hid_relu, 2 * k + t - 1)
                    mm(b_t[:, t * 512:(t + 1) * 512], mw1[:, t * 128:(t + 1) * 128],
                       rp[:, k * 512:(k + 1) * 512], start=True, stop=True).then_inc(hid_mm, 1)
            pe.wait_ge(hid_relu, 2 * (N * N // 512))
            for m in range(N):
                for t in range(2):
                    for side in range(2):
                        mm(b_q[side * N:(side + 1) * N, m * NH:(m + 1) * NH], hid[:, t, m * N:(m + 1) * N],
                           mw2[:, t, :], start=(m == 0 and t == 0), stop=False, skip_group_check=True)
            mm(b_q[:, 0:N * NH], ones[0:1, :], mb2, start=False, stop=True,
               skip_group_check=True).then_inc(pos_mm, 1)
            for t in range(NT):
                pe.wait_ge(gsel_done, t + 1)
                rhs = gsel[:, :, :].rearrange("p s i -> p (s i)")
                if t:
                    pe.wait_ge(spread_out, t)
                mm(b_v[:, 0:2 * NIMG], spread[:, 0:CA], rhs, start=True, stop=True)
                mm(b_v[:, 64:64 + 2 * NIMG], spread[:, CA:256], rhs, start=True, stop=True).then_inc(spread_mm, 1)

            def bias(b):
                pe.wait_ge(norm0_w, b + 1)
                for o, lo in zip(half, (0, HALF)):
                    m = mm(o, ones[0:1, :], qkvb[:, lo:lo + HALF], start=True, stop=False)
                    if lo == 0:
                        m.then_inc(z_free, 1)
                    mm(o, negmean[:, 0, :], wn[:, 0, lo:lo + HALF], start=False, stop=False)
                    last = mm(o, negmean[0:CB, 1, :], wn[0:CB, 1, lo:lo + HALF], start=False, stop=True)
                last.then_inc(bias_mm, 1)

            bias(0)
            with pe.Fori(0, B) as b:
                pe.wait_ge(bias_done, b + 1)

                def stages(j, g, s, on):
                    if on(3):
                        pe.wait_ge(norm_done, g - 2)
                        if on(4):
                            pe.wait_ge(yT_out, g - 3)
                        for t in range(3):
                            last = nc.tensor.transpose(
                                b_p[:, t * 128:(t + 1) * 128],
                                probs[:, (j - 3) % 2, 2 * t:2 * t + 2, :].rearrange("p h m -> p (h m)"), ident[:, :])
                        last.then_inc(pT_mm, 1)
                    if on(0):
                        pe.wait_ge(xh_done, g + 1)
                        e = j % 2
                        products = [(xh[:, e, :], wnh, 0), (xh[:, e, :], wnl, 0), (xhb[:, e, :], wnh, 1),
                                    (xl[:, e, :], wnh, 0), (xhl[:, e, :], wnl, 1)]
                        for o, lo in zip(half, (0, HALF)):
                            if lo and on(1):
                                pe.wait_ge(vT_out, g)
                            for n, (xx, ww, t) in enumerate(products):
                                if not lo and n == 3:
                                    pe.wait_ge(xl_done, g + 1)
                                    pe.wait_ge(xhl_done, g + 1)
                                last = mm(o, xx, ww[:, t, lo:lo + HALF], start=(n == 0), stop=(n == 4))
                        last.then_inc(qkv_mm, 1)
                    if on(4):
                        pe.wait_ge(yT_out, g - 3)
                        if on(5):
                            pe.wait_ge(x1_done, g - 4)
                        ya = yT[:, 0:128].rearrange("p (w r c) -> p r w c", w=2, c=WS)
                        yb = yT[0:CB, 128:256].rearrange("p (w r c) -> p r w c", w=2, c=WS)
                        mm(b_r[:, 0:128], wp[:, 0, 0:CA], ya, start=True, stop=False)
                        mm(b_r[:, 0:128], wp[0:CB, 1, 0:CA], yb, start=False, stop=True)
                        mm(b_r[0:CB, 128:256], wp[:, 0, CA:C], ya, start=True, stop=False)
                        mm(b_r[0:CB, 128:256], wp[0:CB, 1, CA:C], yb, start=False, stop=True).then_inc(proj_mm, 1)
                    if on(1):
                        pe.wait_ge(prod_done, g * 2)
                        if on(2):
                            pe.wait_ge(oT_out, g - 1)
                        for t in range(3):
                            last = mm(b_o[:, t * N:(t + 1) * N],
                                      prod[:, t, :, :, :].rearrange("p h w d -> p (h w d)"), inv[:, :],
                                      start=True, stop=True)
                        last.then_inc(o_mm, 1)
                    if on(0):
                        for win in range(2):
                            pe.wait_ge(lo_out, g * 2 + win + 1)
                            if win and not on(1):
                                pe.wait_ge(v_out, g + 1)
                            o = b_t[0:NF, win * 512:win * 512 + 2 * C]
                            mm(o, fwdh[:, :], qk[:, win, :], start=True, stop=False)
                            mm(o, fwdl[:, :], qk[:, win, :], start=False, stop=True).then_inc(t_mm, 1)
                    if on(3):
                        pe.wait_ge(pT_out, g - 2)
                        pe.wait_ge(vbd_act, g - 2)
                        pe.wait_ge(vbd_dve, g - 2)
                        for t in range(3):
                            p, c = (t % 2) * 64, (t // 2) * 128
                            for win in range(2):
                                last = mm(b_p[p:p + 64, c + win * N:c + (win + 1) * N], vbd[:, (j - 3) % 4, win, t, :],
                                          probsT[:, t, win, :], start=True, stop=True)
                        last.then_inc(y_mm, 1)
                    if on(1):
                        pe.wait_ge(vT_out, g)
                        pe.wait_ge(oT_out, g)
                        if on(2):
                            pe.wait_ge(s_out, g - 1)
                        if on(0):
                            pe.wait_ge(v_out, g + 1)
                        for t in range(3):
                            last = mm(b_s[:, t * 128:(t + 1) * 128], obd[:, t, :, :].rearrange("p w n -> p (w n)"),
                                      vT[:, t, :, :].rearrange("p h m -> p (h m)"), start=True, stop=True)
                        last.then_inc(s_mm, 1)
                    if on(0):
                        for t in range(3):
                            last = nc.tensor.transpose(
                                b_v[:, HALF + t * N:HALF + (t + 1) * N],
                                vt[:, j % 2, t, :, :, :].rearrange("p h w d -> p (h w d)"), ident[0:N, 0:N])
                        last.then_inc(vT_mm, 1)

                pair_loop(pe, b, stages)

                def channels(weights, field, width):
                    rhs = sm[:, field:field + width, :]
                    mm(b_v[:, 0:width], weights[:, 0, 0:CA], rhs[:, :, 0], start=True, stop=False)
                    mm(b_v[:, 0:width], weights[0:CB, 1, 0:CA], rhs[0:CB, :, 1], start=False, stop=True)
                    mm(b_v[0:CB, 64:64 + width], weights[:, 0, CA:C], rhs[:, :, 0], start=True, stop=False)
                    return mm(b_v[0:CB, 64:64 + width], weights[0:CB, 1, CA:C], rhs[0:CB, :, 1], start=False, stop=True)

                pe.wait_ge(st_mean, b + 1)
                channels(mates, 0, 2).then_inc(mean_mm, 1)
                pe.wait_ge(st_dev, b + 1)
                channels(mates, 4, 1).then_inc(dev_mm, 1)
                pe.wait_ge(norm1_w, b + 1)
                channels(mn, 2, 1).then_inc(mbias_mm, 1)

                def merge(k, n, q, first):
                    pe.wait_ge(z_done, n + 1)
                    pe.wait_ge(under_done, n + 1)
                    if not first:
                        pe.wait_ge(fin_a, n - 1)
                        pe.wait_ge(fin_b, n - 1)
                    mm(b_t[:, k * 512:k * 512 + CE], mn[:, 0, 0:CA], z(0, k), start=True, stop=False)
                    mm(b_t[:, k * 512:k * 512 + CE], mn[0:CB, 1, 0:CA], z(1, k), start=False, stop=True)
                    mm(b_s[0:CB, k * 512:k * 512 + CE], mn[:, 0, CA:C], z(0, k), start=True, stop=False)
                    mm(b_s[0:CB, k * 512:k * 512 + CE], mn[:, 1, CA:C], xs[:, 1, 0, k * CE:(k + 1) * CE],
                       start=False, stop=True).then_inc(merge_mm, 1)

                chunk_loop(pe, b, merge)
                bias(b + 1)

        @block.vector
        def _(dve):
            V = nc.vector
            chain = [0, 0]

            def link(ins):
                chain[1] += 1
                ins.then_inc(dve_chain, 1)
                dve.wait_ge(dve_chain, chain[0] + chain[1])

            def rstd(var, sd, r, t, wait):
                link(V.tensor_scalar(var, var, EPS, None, ALU.add))
                V.tensor_copy(t, var).then_inc(var_done, 1)
                dve.wait_ge(sqrt_done, wait)
                link(V.reciprocal(r, sd))
                link(V.tensor_tensor(t, var, r, ALU.mult))
                link(V.tensor_tensor(t, t, r, ALU.mult))
                link(V.tensor_scalar(t, t, -0.5, 1.5, ALU.mult, ALU.add))
                link(V.tensor_tensor(r, r, t, ALU.mult))

            dve.wait_ge(const_in, 16 * len(loads))
            dve.wait_ge(sbuf_zero, 1)
            V.tensor_copy(mn[CB:128, 1, CA:C], ident[CB:128, CB:128])
            link(V.tensor_copy(fwdh[:, :], fwd))
            V.tensor_tensor(fwdl[:, :], fwd, fwdh[:, :].bitcast(F32), ALU.subtract)
            V.tensor_scalar(wnh[CB:128, 1, :], ones[CB:128, 0:1].broadcast_to([CB, 3 * C]), 0.0, None, ALU.mult)
            for e in range(2):
                last = V.tensor_scalar(xhb[CB:128, e, :], ones[CB:128, :], 0.0, None, ALU.mult)
            link(last)
            for e in range(2):
                for row in BIAS_ROWS:
                    last = V.tensor_copy(xhb[row:row + 1, e, :], ones[row:row + 1, :])
            link(last)
            for t in range(NT):
                for c in range(NL):
                    n = t * NL + c
                    dve.wait_ge(ld_in[n % NLOAD], 16 * (n // NLOAD + 1))
                    for i in range(LOAD // STAT):
                        last = V.bn_stats(bn0[:, c * (LOAD // STAT) + i, :], ld[:, n % NLOAD, i * STAT:(i + 1) * STAT])
                    last.then_inc(ld_read, 1)
                dve.wait_ge(ld_read, (t + 1) * NL)
                link(V.bn_aggr(gst[:, 0:2], bn0[:, :, :].rearrange("p k n -> p (k n)")))
                rstd(gst[:, 1:2], gst[:, 2:3], gst[:, 3:4], gst[:, 4:5], t + 1)
                V.tensor_scalar(gsel[:, 0, :], image[:, :], gst[:, 0:1], None, ALU.mult)
                V.tensor_scalar(gsel[:, 1, :], image[:, :], gst[:, 3:4], None, ALU.mult).then_inc(gsel_done, 1)
                dve.wait_ge(spread_mm, t + 1)
                to = st0[:, :, :, t * NIMG:(t + 1) * NIMG]
                V.tensor_copy(to[:, 0], b_v[:, 0:2 * NIMG].rearrange("p (s i) -> p s i", s=2))
                link(V.tensor_copy(to[:, 1], b_v[:, 64:64 + 2 * NIMG].rearrange("p (s i) -> p s i", s=2)))
                if t + 1 < NT:
                    V.tensor_copy(gst[:, 7:8], gst[:, 0:1]).then_inc(spread_out, 1)
            dve.wait_ge(pos_mm, 1)
            link(V.tensor_copy(posb[:, :, :], b_q[:, 0:N * NH].rearrange("p (m h) -> p h m", h=NH)))

            def weights(b):
                for t in range(2):
                    last = V.tensor_scalar(wn[:, t, :], wq[:, t, :], st0[:, t, 1, bass.ds(b, 1)], None, ALU.mult)
                link(last)
                V.tensor_copy(wnh[:, 0, :], wn[:, 0, :])
                V.tensor_copy(wnh[0:CB, 1, :], wn[0:CB, 1, :])
                link(V.tensor_copy(wnl[CB:128, 1, :], wn[CB:128, 1, :]))
                V.tensor_tensor(wnl[:, 0, :], wn[:, 0, :], wnh[:, 0, :].bitcast(F32), ALU.subtract)
                V.tensor_tensor(wnl[0:CB, 1, :], wn[0:CB, 1, :], wnh[0:CB, 1, :].bitcast(F32), ALU.subtract)
                for t in range(2):
                    last = V.tensor_scalar(negmean[:, t, :], ones[:, :], st0[:, t, 0, bass.ds(b, 1)], -1.0,
                                           ALU.mult, ALU.mult)
                last.then_inc(norm0_w, 1)

            def bias(b):
                dve.wait_ge(bias_mm, b + 1)
                first, second = (slice(row, row + 1) for row in BIAS_ROWS)
                halves = "p (k c) -> p k c"
                V.tensor_copy(wnh[first, 1, :].rearrange(halves, k=2), b_q[first].rearrange(halves, k=2)[:, :, 0:HALF])
                link(V.tensor_copy(biasrow[second].bitcast(F32R).rearrange(halves, k=2),
                                   b_q[second].rearrange(halves, k=2)[:, :, 0:HALF]))
                link(V.tensor_tensor(wnh[second, 1, :].rearrange(halves, k=2),
                                     b_q[second].rearrange(halves, k=2)[:, :, 0:HALF],
                                     biasrow[second].rearrange(halves, k=2), ALU.subtract))
                V.tensor_copy(biasrow[0:1, 0:1], ones[0:1, 0:1]).then_inc(bias_done, 1)

            weights(0)
            bias(0)
            chained = chain[1]

            with dve.Fori(0, B) as b:
                PER_IMAGE = 17
                chain[0], chain[1] = b * PER_IMAGE, chained

                def tokens(win):
                    return slice(win * N, (win + 1) * N)

                def stages(j, g, s, on):
                    if on(0):
                        vv = vt[:, j % 2, :, :, :, :]

                        def values(win):
                            return V.tensor_copy(
                                vv[:, :, :, win, :].rearrange("p t h d -> p (t h) d")
                                .rearrange("p (k x) d -> p k x d", k=2),
                                b_q[tokens(win)].rearrange("p (k c) -> p k c", k=2)[:, :, C:HALF]
                                .rearrange("p k (x d) -> p k x d", d=HD))

                        def rest(win):
                            dve.wait_ge(hi_out, g * 2 + win + 1)
                            V.tensor_tensor(qk[tokens(1 - win), win, :].rearrange("p (k c) -> p k c", k=2),
                                            b_q[tokens(win)].rearrange("p (k c) -> p k c", k=2)[:, :, 0:C],
                                            qk[tokens(win), win, :].bitcast(F32).rearrange("p (k c) -> p k c", k=2),
                                            ALU.subtract).then_inc(lo_out, 1)

                        dve.wait_ge(qkv_mm, g + 1)
                        values(1).then_inc(v1_out, 1)
                        rest(0)
                        rest(1)
                    if on(2):
                        dve.wait_ge(exp_done, g - 1)
                        V.tensor_reduce(ssum[:, j % 2, :], probs[:, j % 2, :, :], AX.X, ALU.add
                                        ).then_inc(sum_done, 1)
                    if on(0):
                        values(0).then_inc(v_out, 1)
                    if on(2):
                        dve.wait_ge(sum_done, g - 1)
                        V.reciprocal(srec[:, j % 2, :], ssum[:, j % 2, :]).then_inc(rec_done, 1)

                    if on(4):
                        i = j - 4
                        row, col, k = (s + i // SPAIRS) * WS + 1, (i % SPAIRS) * 16, (i % UN) // SPAIRS
                        dve.wait_ge(proj_mm, g - 3)
                        for t, n, xt in ((0, CA, x1a), (1, CB, x1b)):
                            last = V.scalar_tensor_tensor(
                                out=xt[:, bass.ds(row, WS), col + 1:col + 17],
                                in0=b_r[0:n, t * 128:(t + 1) * 128].rearrange("p (r c) -> p r c", c=16),
                                scalar=pb[0:n, t:t + 1],
                                in1=xs[0:n, t, k, :].rearrange("p (r c) -> p r c", c=W)[:, :, col:col + 16],
                                op0=ALU.add, op1=ALU.add)
                        last.then_inc(x1_done, 1)
                    final = not on(0) and j == 3
                    for part in range(8):
                        i = j - 4 if final else j - 4 - part
                        if i % SPAIRS == SPAIRS - 1 and on(j - i):
                            if part == 0:
                                dve.wait_ge(x1_done, g - 3)
                            t, q = part // 4, part % 4
                            n, xt = ((CA, x1a), (CB, x1b))[t]
                            strip = s + i // SPAIRS
                            V.bn_stats(bn1[0:n, t, bass.ds(strip * 4 + q, 1), :],
                                       xt[:, bass.ds(strip * WS + q * 2 + 1, 2), 1:W + 1])

                def late(j, g, s, on):
                    if on(1):
                        pr = probs[:, (j - 1) % 2, :, :]
                        dve.wait_ge(s_mm, g)
                        V.tensor_tensor(pr, b_s[:, 0:NH * N].rearrange("p (h m) -> p h m", m=N), posb[:, :, :],
                                        ALU.add).then_inc(s_out, 1)
                    if on(0):
                        dve.wait_ge(v_out, g + 1)
                        V.tensor_copy(vbd[0:N, j % 4, :, :, 0:HD],
                                      vt[:, j % 2, :, 0, :, :].rearrange("p t w d -> p w t d")).then_inc(vbd_dve, 1)
                    if on(1):
                        dve.wait_ge(s_out, g)
                        V.tensor_reduce(smax[:, (j - 1) % 2, :], pr, AX.X, ALU.max).then_inc(max_done, 1)
                    if on(0):
                        for win in range(2):
                            dve.wait_ge(qh_out, g * 2 + win + 1)
                            V.tensor_tensor(prod[:, :, :, win, :].rearrange("p t h d -> p (t h) d"),
                                            qh[:, win, :].rearrange("p (h d) -> p h d", d=HD),
                                            b_t[0:NF, win * 512 + C:win * 512 + 2 * C]
                                            .rearrange("p (h d) -> p h d", d=HD), ALU.mult).then_inc(prod_done, 1)

                def second_part(j, g, s, on):
                    k, c = j // SPAIRS, (j % SPAIRS) * 2
                    dve.wait_ge(xh_done, g + 1)
                    V.tensor_tensor(xhl[CB:128, j % 2, :].rearrange("p (w r c) -> p w r c", w=2, c=WS),
                                    pixels(1, k, c),
                                    xhl[0:CB, j % 2, :].bitcast(F32).rearrange("p (w r c) -> p w r c", w=2, c=WS),
                                    ALU.subtract).then_inc(xhl_done, 1)

                pair_loop(dve, b, ahead(stages, second_part, late), LAST + 1)

                link(V.memset(sm[:, 7, :], 0.0))
                V.memset(sm[:, 6, :], 0.0)
                for t, n in ((0, CA), (1, CB)):
                    last = V.bn_aggr(sm[0:n, 0:2, t], bn1[0:n, t, :, :].rearrange("p k n -> p (k n)"))
                last.then_inc(st_mean, 1)
                dve.wait_ge(mean_mm, b + 1)
                V.tensor_copy(sm[:, 2:4, 0], b_v[:, 0:2])
                link(V.tensor_copy(sm[0:CB, 2:4, 1], b_v[0:CB, 64:66]))
                link(V.tensor_tensor(sm[:, 4, :], sm[:, 0, :], sm[:, 2, :], ALU.subtract))
                V.tensor_tensor(sm[:, 4, :], sm[:, 4, :], sm[:, 4, :], ALU.mult).then_inc(st_dev, 1)
                for t, n, xt in ((0, CA, x1a), (1, CB, x1b)):
                    for edge in (0, PW - 1):
                        V.tensor_scalar(xt[:, :, edge], ones[0:n, 0:1].broadcast_to([n, H + 2]), sm[0:n, 2, t:t + 1],
                                        None, ALU.mult)
                    for edge in (0, H + 1):
                        last = V.tensor_scalar(xt[:, edge, 1:PW - 1], ones[0:n, 0:1].broadcast_to([n, W]),
                                               sm[0:n, 2, t:t + 1], None, ALU.mult)
                last.then_inc(border_w, 1)
                dve.wait_ge(dev_mm, b + 1)
                link(V.tensor_tensor(sm[:, 5, 0:1], b_v[:, 0:1], sm[:, 3, 0:1], ALU.add))
                link(V.tensor_tensor(sm[0:CB, 5, 1:2], b_v[0:CB, 64:65], sm[0:CB, 3, 1:2], ALU.add))
                rstd(sm[:, 5, :], sm[:, 6, :], sm[:, 7, :], sm[:, 4, :], b + NT + 1)
                for t, n in ((0, CA), (1, CB)):
                    last = V.tensor_scalar(mn[0:n, t, :], wm[0:n, t, :], sm[0:n, 7, t:t + 1], None, ALU.mult)
                last.then_inc(norm1_w, 1)
                def neighbours(k, n, q):
                    dve.wait_ge(diag_done, n + 1)
                    for t, m in ((0, CA), (1, CB)):
                        dg = diag[0:m, t, k, :, :]
                        last = V.tensor_tensor(z(t, k).rearrange("p (r c) -> p r c", c=W), dg[:, 0:ROWS, 0:W],
                                               dg[:, 1:, 1:], ALU.add)
                    last.then_inc(nb_done, 1)

                def stencil(k, n, q):
                    dve.wait_ge(nb_done, n + 1)
                    for t, xt in ((0, x1a), (1, x1b)):
                        zz = z(t, k).rearrange("p (r c) -> p r c", c=W)
                        last = V.scalar_tensor_tensor(out=zz, in0=xt[:, bass.ds(q * ROWS + 1, ROWS), 1:W + 1], scalar=5.0,
                                                      in1=zz, op0=ALU.mult, op1=ALU.subtract)
                    last.then_inc(z_done, 1)

                def result(k, n, q):
                    dve.wait_ge(merge_mm, n + 1)
                    if not (isinstance(q, int) and q < 2):
                        dve.wait_ge(out_sent[k], n * 16 - k * 16 + 1)
                    V.scalar_tensor_tensor(
                        out=res(0, k).rearrange("p (r c) -> p r c", c=W),
                        in0=b_t[:, k * 512:k * 512 + CE].rearrange("p (r c) -> p r c", c=W),
                        scalar=mc[:, 0:1], in1=x1a[:, bass.ds(q * ROWS + 1, ROWS), 1:W + 1],
                        op0=ALU.add, op1=ALU.add).then_inc(fin_a, 1)

                n0 = b * NCH
                for k in range(2):
                    neighbours(k, n0 + k, k)
                    stencil(k, n0 + k, k)
                dve.wait_ge(mbias_mm, b + 1)
                link(V.tensor_tensor(mc[:, 0:1], mb[:, 0:1], b_v[:, 0:1], ALU.subtract))
                link(V.tensor_tensor(mc[0:CB, 1:2], mb[0:CB, 1:2], b_v[0:CB, 64:65], ALU.subtract))
                V.tensor_copy(sm[:, 4, :], mc[:, :]).then_inc(mc_done, 1)
                for k in range(2):
                    dve.wait_ge(merge_mm, n0 + k + 1)
                    neighbours(k, n0 + 2 + k, 2 + k)
                    result(k, n0 + k, k)
                    stencil(k, n0 + 2 + k, 2 + k)
                with dve.Fori(0, NCH // 4 - 1) as d:
                    for k in range(4):
                        n, q = n0 + d * 4 + (k + 2), d * 4 + (k + 2)
                        dve.wait_ge(merge_mm, n + 1)
                        neighbours(k % 2, n + 2, q + 2)
                        result(k % 2, n, q)
                        stencil(k % 2, n + 2, q + 2)
                weights(b + 1)
                for k in range(2):
                    result(k, n0 + NCH - 2 + k, NCH - 2 + k)
                bias(b + 1)
                assert chain[1] - chained == PER_IMAGE

        @block.scalar
        def _(act):
            A = nc.scalar

            def copy(o, i):
                return A.activation(o, i, ACT.Copy)

            for k in range(N * N // 512):
                for t in range(2):
                    act.wait_ge(hid_mm, 2 * k + t + 1)
                    A.activation(hid[:, t, k * 512:(k + 1) * 512], b_t[:, t * 512:(t + 1) * 512], ACT.Relu,
                                 bias=mb1[:, t:t + 1]).then_inc(hid_relu, 1)
            for t in range(NT):
                act.wait_ge(var_done, t + 1)
                A.activation(gst[:, 2:3], gst[:, 1:2], ACT.Sqrt).then_inc(sqrt_done, 1)

            act.wait_ge(sbuf_zero, 1)
            with act.Fori(0, B) as b:
                def first_part(j, g, s, on):
                    k, c = j // SPAIRS, (j % SPAIRS) * 2
                    if j % SPAIRS == 0:
                        act.wait_ge(strip_in[k], b * (NB * 32) + s * 16 + 32)
                    if on(2):
                        act.wait_ge(qkv_mm, g - 1)
                    for t, o in ((0, xh), (1, xhb), (1, xhl)):
                        last = copy(o[0:CA if t == 0 else CB, j % 2, :].rearrange("p (w r c) -> p w r c", w=2, c=WS),
                                    pixels(t, k, c))
                    last.then_inc(xh_done, 1)

                def stages(j, g, s, on):
                    if on(3):
                        act.wait_ge(pT_mm, g - 2)
                        copy(probsT[:, :, :, :].rearrange("p t w n -> p (t w n)"), b_p[:, 0:NH * N]).then_inc(pT_out, 1)
                    if on(0):
                        act.wait_ge(qkv_mm, g + 1)
                        for win in range(2):
                            if win:
                                act.wait_ge(v1_out, g + 1)
                            rows = slice(win * N, (win + 1) * N)
                            copy(qk[rows, win, :].rearrange("p (k c) -> p k c", k=2),
                                 b_q[rows].rearrange("p (k c) -> p k c", k=2)[:, :, 0:C]).then_inc(hi_out, 1)
                    if on(2):
                        act.wait_ge(sub_done, g - 1)
                        pr = probs[:, j % 2, :, :].rearrange("p h m -> p (h m)")
                        A.activation(pr, pr, ACT.Exp).then_inc(exp_done, 1)
                    if on(1):
                        act.wait_ge(o_mm, g)
                        for p in range(0, 128, HD):
                            last = copy(obd[p:p + HD, :, p // HD % 2, :],
                                        b_o[p:p + HD, 0:3 * N].rearrange("p (t n) -> p t n", n=N))
                        last.then_inc(oT_out, 1)

                def late(j, g, s, on):
                    if on(3):
                        act.wait_ge(y_mm, g - 2)
                        copy(yT[:, :], b_p[:, 0:256]).then_inc(yT_out, 1)
                    if on(0):
                        for win in range(2):
                            act.wait_ge(t_mm, g * 2 + win + 1)
                            copy(qh[:, win, :], b_t[0:NF, win * 512:win * 512 + C]).then_inc(qh_out, 1)
                    if on(0):
                        act.wait_ge(vT_mm, g + 1)
                        for h in range(2):
                            rows = slice(h * 64, h * 64 + 64)
                            last = copy(vT[rows, :, h, :],
                                        b_v[rows, HALF:HALF + 3 * N].rearrange("p (t m) -> p t m", m=N))
                        last.then_inc(vT_out, 1)
                        act.wait_ge(v_out, g + 1)
                        copy(vbd[N:128, j % 4, :, :, HD:], vt[:, j % 2, :, 1, :, :].rearrange("p t w d -> p w t d")
                             ).then_inc(vbd_act, 1)

                pair_loop(act, b, ahead(stages, first_part, late), LAST + 1)
                act.wait_ge(var_done, b + NT + 1)
                A.activation(sm[:, 6, :], sm[:, 5, :], ACT.Sqrt).then_inc(sqrt_done, 1)

                def under(k, n, q):
                    copy(x1_under(k).rearrange("p (r c) -> p r c", c=W), x1b[:, bass.ds(q * ROWS + 1, ROWS), 1:W + 1]
                         ).then_inc(under_done, 1)

                def result(k, n, q):
                    if not (isinstance(q, int) and q < 2):
                        act.wait_ge(out_sent[k], n * 16 - k * 16 + 1)
                    A.activation(res(1, k), b_s[0:CB, k * 512:k * 512 + CE], ACT.Identity, bias=mc[0:CB, 1:2]
                                 ).then_inc(fin_b, 1)

                n0 = b * NCH
                for k in range(2):
                    under(k, n0 + k, k)
                act.wait_ge(mc_done, b + 1)
                for k in range(2):
                    act.wait_ge(merge_mm, n0 + k + 1)
                    under(k, n0 + 2 + k, 2 + k)
                    result(k, n0 + k, k)
                with act.Fori(0, NCH // 4 - 1) as d:
                    for k in range(4):
                        n, q = n0 + d * 4 + (k + 2), d * 4 + (k + 2)
                        act.wait_ge(merge_mm, n + 1)
                        under(k % 2, n + 2, q + 2)
                        result(k % 2, n, q)
                for k in range(2):
                    act.wait_ge(merge_mm, n0 + NCH - 1 + k)
                    result(k, n0 + NCH - 2 + k, NCH - 2 + k)

        @block.gpsimd
        def _(pool):
            P = nc.gpsimd
            pool.wait_ge(const_in, 16 * len(loads))
            P.memset(ones[:, :], 1.0)
            P.memset(obd[:, :, :, :], 0.0)
            P.memset(vT[:, :, :, :], 0.0)
            P.memset(st0[:, :, :, :], 0.0)
            P.memset(mc[:, :], 0.0)
            P.memset(sm[:, :, :], 0.0)
            P.memset(vbd[:, :, :, :, :], 0.0).then_inc(sbuf_zero, 1)
            with pool.Fori(0, B) as b:
                def stages(j, g, s, on):
                    if on(2):
                        pr = probs[:, j % 2, :, :]
                        pool.wait_ge(max_done, g - 1)
                        P.tensor_tensor(pr, pr, smax[:, j % 2, :].unsqueeze(2).broadcast_to([128, NH, N]),
                                        ALU.subtract).then_inc(sub_done, 1)
                        pool.wait_ge(rec_done, g - 1)
                        P.tensor_tensor(pr, pr, srec[:, j % 2, :].unsqueeze(2).broadcast_to([128, NH, N]),
                                        ALU.mult).then_inc(norm_done, 1)

                def second_part(j, g, s, on):
                    k, c = j // SPAIRS, (j % SPAIRS) * 2
                    pool.wait_ge(xh_done, g + 1)
                    P.tensor_tensor(xl[:, j % 2, :].rearrange("p (w r c) -> p w r c", w=2, c=WS), pixels(0, k, c),
                                    xh[:, j % 2, :].bitcast(F32).rearrange("p (w r c) -> p w r c", w=2, c=WS),
                                    ALU.subtract).then_inc(xl_done, 1)

                pair_loop(pool, b, ahead(stages, second_part, lambda *a: None), LAST + 1)
                pool.wait_ge(border_w, b + 1)

                def diagonals(k, n, q, first):
                    if not first:
                        pool.wait_ge(nb_done, n - 1)
                    for t, m, xt in ((0, CA, x1a), (1, CB, x1b)):
                        last = P.tensor_tensor(diag[0:m, t, k, :, :], xt[:, bass.ds(q * ROWS + 1, ROWS + 1), 0:W + 1],
                                               xt[:, bass.ds(q * ROWS, ROWS + 1), 1:W + 2], ALU.add)
                    last.then_inc(diag_done, 1)

                chunk_loop(pool, b, diagonals)


def halves(qk, v):
    return np.concatenate([qk[:C], v[:C // 2], qk[C:], v[C // 2:]])


def kernel(**inputs):
    import concourse.bacc as bacc
    from concourse.bass_utils import run_bass_kernel_spmd

    a = {k: np.asarray(v) for k, v in inputs.items()}
    x = a["x"]
    arrays = {
        "x": x,
        "wqkvT": np.ascontiguousarray(halves(a["L0_conv_QK_w"], a["L0_conv_V_w"]).T),
        "qkvb": halves(a["L0_conv_QK_b"], a["L0_conv_V_b"])[None],
        "projT": np.ascontiguousarray(a["L0_conv_proj_w"].T),
        "projb": a["L0_conv_proj_b"][:, None],
        "mergeT": np.ascontiguousarray(a["L1_conv_merge_w"][:, :, 0, 0].T),
        "mergeb": a["L1_conv_merge_b"][:, None],
        "w1": a["L0_conv_meta_w1"],
        "b1": np.ascontiguousarray(a["L0_conv_meta_b1"].reshape(-1, 128).T),
        "w2": a["L0_conv_meta_w2"],
        "b2": np.tile(a["L0_conv_meta_b2"], N)[None],
    }
    for name, value in constants(x.shape[0]).items():
        arrays[name] = np.ascontiguousarray(value, dtype=np.float32)
    nc = bacc.Bacc("TRN2", target_bir_lowering=False, num_devices=1)
    w = {name: nc.dram_tensor("in_" + name, value.shape, F32, kind="ExternalInput").ap()
         for name, value in arrays.items()}
    out = nc.dram_tensor("out", x.shape, F32, kind="ExternalOutput").ap()
    program(nc, w["x"], out, w)
    r = run_bass_kernel_spmd(nc, [{"in_" + name: value for name, value in arrays.items()}], core_ids=[0])
    return r.results[0]["out"]
```
